# Optimizing a Trainium2 kernel written in Bass

```python
import numpy as np
import jax
import jax.numpy as jnp

def _softmax(x, axis=-1):
    return jax.nn.softmax(x, axis=axis)
def _gelu(x):
    return jax.nn.gelu(x, approximate=True)
def _silu(x):
    return jax.nn.silu(x)
def _sigmoid(x):
    return jax.nn.sigmoid(x)
def _layernorm(x, axis=-1, eps=1e-5):
    m = jnp.mean(x, axis=axis, keepdims=True)
    v = jnp.var(x, axis=axis, keepdims=True)
    return (x - m) / jnp.sqrt(v + eps)
def _scatter_add(tgt, idx, src, axis=0):
    return tgt.at[idx].add(src)
def _segment_sum(src, seg, n):
    return jax.ops.segment_sum(src, seg, n)

kernel_name = 'mk_conv_seq_d2_conv_nchw512_25f242'

def setup_inputs(seed: int = 0):
    np.random.seed(seed)
    _w = jnp.asarray
    def _rec_inputs():
        import jax
        import jax.numpy as jnp
        _gk = jax.random.key(seed)
        x = -0.0002928 + 1 * jax.random.normal(jax.random.fold_in(_gk, 1), (8, 512, 32, 32), jnp.float32)
        return x
    x = _rec_inputs()
    def _L0_conv_setup():
        import jax, jax.numpy as jnp
        import numpy as np
        NUM_HEADS = 8
        NUM_GROUPS = 32
        EPS = 1e-05

        def group_norm(x, gamma, beta):
            B, C, H, W = x.shape
            xg = x.reshape(B, NUM_GROUPS, C // NUM_GROUPS * H * W)
            mean = xg.mean(axis=-1, keepdims=True)
            var = xg.var(axis=-1, keepdims=True)
            xg = (xg - mean) * jax.lax.rsqrt(var + EPS)
            xn = xg.reshape(B, C, H, W)
            return xn * gamma[None, :, None, None] + beta[None, :, None, None]
        key = jax.random.key(seed)
        ks = jax.random.split(key, 7)
        C = 512
        B, H, W = (8, 32, 32)
        x = jax.random.normal(ks[0], (B, C, H, W), dtype=jnp.float32)
        gamma = jnp.ones((C,), dtype=jnp.float32)
        beta = jnp.zeros((C,), dtype=jnp.float32)
        w_qkv = jax.random.normal(ks[1], (3 * C, C), dtype=jnp.float32) * (1.0 / np.sqrt(C))
        b_qkv = jax.random.normal(ks[2], (3 * C,), dtype=jnp.float32) * 0.02
        w_proj = jax.random.normal(ks[3], (C, C), dtype=jnp.float32) * (1.0 / np.sqrt(C))
        b_proj = jax.random.normal(ks[4], (C,), dtype=jnp.float32) * 0.02
        return {'x': x, 'gamma': gamma, 'beta': beta, 'w_qkv': w_qkv, 'b_qkv': b_qkv, 'w_proj': w_proj, 'b_proj': b_proj}
    _L0_conv_all = _L0_conv_setup()
    _L0_conv_in = {k: v for k, v in _L0_conv_all.items() if k in ('gamma', 'beta', 'w_qkv', 'b_qkv', 'w_proj', 'b_proj', )}
    del _L0_conv_all

    def _L1_conv_setup():
        import jax, jax.numpy as jnp
        import numpy as np
        NUM_GROUPS = 32
        EPS = 1e-06

        def group_norm(x, gamma, beta):
            b, c, h, w = x.shape
            xg = x.reshape(b, NUM_GROUPS, c // NUM_GROUPS, h, w)
            mean = xg.mean(axis=(2, 3, 4), keepdims=True)
            var = xg.var(axis=(2, 3, 4), keepdims=True)
            xg = (xg - mean) * jax.lax.rsqrt(var + EPS)
            x = xg.reshape(b, c, h, w)
            return x * gamma[None, :, None, None] + beta[None, :, None, None]

        def conv1x1(x, w, bias):
            return jnp.einsum('bchw,oc->bohw', x, w) + bias[None, :, None, None]
        key = jax.random.key(seed)
        ks = jax.random.split(key, 6)
        B, C, H, W = (1, 512, 96, 96)
        std = 1.0 / np.sqrt(C)
        return {'x': jax.random.normal(ks[0], (B, C, H, W), dtype=jnp.float32), 'gn_gamma': jnp.ones((C,), dtype=jnp.float32), 'gn_beta': jnp.zeros((C,), dtype=jnp.float32), 'q_w': jax.random.normal(ks[1], (C, C), dtype=jnp.float32) * std, 'q_b': jnp.zeros((C,), dtype=jnp.float32), 'k_w': jax.random.normal(ks[2], (C, C), dtype=jnp.float32) * std, 'k_b': jnp.zeros((C,), dtype=jnp.float32), 'v_w': jax.random.normal(ks[3], (C, C), dtype=jnp.float32) * std, 'v_b': jnp.zeros((C,), dtype=jnp.float32), 'proj_w': jax.random.normal(ks[4], (C, C), dtype=jnp.float32) * std, 'proj_b': jnp.zeros((C,), dtype=jnp.float32)}
    _L1_conv_all = _L1_conv_setup()
    _L1_conv_in = {k: v for k, v in _L1_conv_all.items() if k in ('gn_gamma', 'gn_beta', 'q_w', 'q_b', 'k_w', 'k_b', 'v_w', 'v_b', 'proj_w', 'proj_b', )}
    del _L1_conv_all

    return {
        "x": x,
        "L0_conv_gamma": _L0_conv_in["gamma"],
        "L0_conv_beta": _L0_conv_in["beta"],
        "L0_conv_w_qkv": _L0_conv_in["w_qkv"],
        "L0_conv_b_qkv": _L0_conv_in["b_qkv"],
        "L0_conv_w_proj": _L0_conv_in["w_proj"],
        "L0_conv_b_proj": _L0_conv_in["b_proj"],
        "L1_conv_gn_gamma": _L1_conv_in["gn_gamma"],
        "L1_conv_gn_beta": _L1_conv_in["gn_beta"],
        "L1_conv_q_w": _L1_conv_in["q_w"],
        "L1_conv_q_b": _L1_conv_in["q_b"],
        "L1_conv_k_w": _L1_conv_in["k_w"],
        "L1_conv_k_b": _L1_conv_in["k_b"],
        "L1_conv_v_w": _L1_conv_in["v_w"],
        "L1_conv_v_b": _L1_conv_in["v_b"],
        "L1_conv_proj_w": _L1_conv_in["proj_w"],
        "L1_conv_proj_b": _L1_conv_in["proj_b"],
    }

def reference(x, L0_conv_gamma, L0_conv_beta, L0_conv_w_qkv, L0_conv_b_qkv, L0_conv_w_proj, L0_conv_b_proj, L1_conv_gn_gamma, L1_conv_gn_beta, L1_conv_q_w, L1_conv_q_b, L1_conv_k_w, L1_conv_k_b, L1_conv_v_w, L1_conv_v_b, L1_conv_proj_w, L1_conv_proj_b):
    import jax
    import jax.numpy as jnp
    def _L0_conv_ref(x, gamma, beta, w_qkv, b_qkv, w_proj, b_proj):
        import jax, jax.numpy as jnp
        import numpy as np
        NUM_HEADS = 8
        NUM_GROUPS = 32
        EPS = 1e-05

        def group_norm(x, gamma, beta):
            B, C, H, W = x.shape
            xg = x.reshape(B, NUM_GROUPS, C // NUM_GROUPS * H * W)
            mean = xg.mean(axis=-1, keepdims=True)
            var = xg.var(axis=-1, keepdims=True)
            xg = (xg - mean) * jax.lax.rsqrt(var + EPS)
            xn = xg.reshape(B, C, H, W)
            return xn * gamma[None, :, None, None] + beta[None, :, None, None]
        B, C, H, W = x.shape
        hd = C // NUM_HEADS
        x_norm = group_norm(x, gamma, beta)
        qkv = jnp.einsum('bchw,oc->bohw', x_norm, w_qkv) + b_qkv[None, :, None, None]
        q, k, v = jnp.split(qkv, 3, axis=1)
        N = H * W
        q = q.reshape(B, NUM_HEADS, hd, N)
        k = k.reshape(B, NUM_HEADS, hd, N)
        v = v.reshape(B, NUM_HEADS, hd, N)
        attn = jnp.einsum('bhcn,bhcm->bhnm', q, k) * hd ** (-0.5)
        attn = jax.nn.softmax(attn, axis=-1)
        out = jnp.einsum('bhnm,bhcm->bhcn', attn, v)
        out = out.reshape(B, C, H, W)
        proj = jnp.einsum('bchw,oc->bohw', out, w_proj) + b_proj[None, :, None, None]
        return x + proj

    def _L1_conv_ref(x, gn_gamma, gn_beta, q_w, q_b, k_w, k_b, v_w, v_b, proj_w, proj_b):
        import jax, jax.numpy as jnp
        import numpy as np
        NUM_GROUPS = 32
        EPS = 1e-06

        def group_norm(x, gamma, beta):
            b, c, h, w = x.shape
            xg = x.reshape(b, NUM_GROUPS, c // NUM_GROUPS, h, w)
            mean = xg.mean(axis=(2, 3, 4), keepdims=True)
            var = xg.var(axis=(2, 3, 4), keepdims=True)
            xg = (xg - mean) * jax.lax.rsqrt(var + EPS)
            x = xg.reshape(b, c, h, w)
            return x * gamma[None, :, None, None] + beta[None, :, None, None]

        def conv1x1(x, w, bias):
            return jnp.einsum('bchw,oc->bohw', x, w) + bias[None, :, None, None]
        b, c, h, w = x.shape
        hn = group_norm(x, gn_gamma, gn_beta)
        q = conv1x1(hn, q_w, q_b).reshape(b, c, h * w)
        k = conv1x1(hn, k_w, k_b).reshape(b, c, h * w)
        v = conv1x1(hn, v_w, v_b).reshape(b, c, h * w)
        scale = jnp.asarray(c, x.dtype) ** (-0.5)
        scores = jnp.einsum('bci,bcj->bij', q, k) * scale
        attn = jax.nn.softmax(scores, axis=-1)
        out = jnp.einsum('bcj,bij->bci', v, attn).reshape(b, c, h, w)
        out = conv1x1(out, proj_w, proj_b)
        return x + out

    def _gn(v, G=32, eps=1e-5):
        B_, C_, H_, W_ = v.shape
        g = v.reshape(B_, G, C_ // G, H_, W_)
        m = jnp.mean(g, axis=(2, 3, 4), keepdims=True)
        s = jnp.var(g, axis=(2, 3, 4), keepdims=True)
        return ((g - m) / jnp.sqrt(s + eps)).reshape(v.shape)

    def _ln_c(v, eps=1e-6):
        m = jnp.mean(v, axis=1, keepdims=True)
        s = jnp.var(v, axis=1, keepdims=True)
        return (v - m) / jnp.sqrt(s + eps)

    def _ln_t(v, eps=1e-5):
        m = jnp.mean(v, axis=-1, keepdims=True)
        s = jnp.var(v, axis=-1, keepdims=True)
        return (v - m) / jnp.sqrt(s + eps)

    def _to_tokens(v):
        B_, C_, H_, W_ = v.shape
        return v.reshape(B_, C_, H_ * W_).transpose(0, 2, 1)
    def _from_tokens(t, like):
        B_, C_, H_, W_ = like.shape
        return t.transpose(0, 2, 1).reshape(B_, C_, H_, W_)

    x = _L0_conv_ref(x, L0_conv_gamma, L0_conv_beta, L0_conv_w_qkv, L0_conv_b_qkv, L0_conv_w_proj, L0_conv_b_proj)
    x = _L1_conv_ref(x, L1_conv_gn_gamma, L1_conv_gn_beta, L1_conv_q_w, L1_conv_q_b, L1_conv_k_w, L1_conv_k_b, L1_conv_v_w, L1_conv_v_b, L1_conv_proj_w, L1_conv_proj_b)
    return x


_drawn_inputs = setup_inputs


def setup_inputs(seed=0):
    import zlib

    import numpy as np

    out = dict(_drawn_inputs(seed))
    spreads = {'L0_conv_gamma': (1.0, 0.2),
     'L0_conv_beta': (0.0, 0.1),
     'L1_conv_gn_gamma': (1.0, 0.2),
     'L1_conv_gn_beta': (0.0, 0.1),
     'L1_conv_q_b': (0.0, 0.8),
     'L1_conv_k_b': (0.0, 0.8),
     'L1_conv_v_b': (0.0, 0.1),
     'L1_conv_proj_b': (0.0, 0.1)}
    factors = {}
    for name, (base, spread) in spreads.items():
        noise = np.random.default_rng([zlib.crc32(name.encode()), seed]).standard_normal(out[name].shape)
        drawn = base * np.exp(spread * noise) if base else spread * noise
        out[name] = jnp.asarray(drawn.astype(out[name].dtype))
    for name, factor in factors.items():
        out[name] = (out[name] * factor).astype(out[name].dtype)
    return out
```

```python
from contextlib import ExitStack

import concourse.bass as bass
from concourse import mybir

ALU = mybir.AluOpType
ACT = mybir.ActivationFunctionType
AX = mybir.AxisListType
F32 = mybir.dt.float32
F32R = mybir.dt.float32r

P = 128
B, C, N = 8, 512, 1024
HEADS, GROUPS = 8, 32
HD = C // HEADS
KT = C // P
MT = N // P
HALF = 512
NH = N // HALF
PAIRS = HEADS // 2
BLK = 2 * MT
GRP = HALF // P
SCALE0 = float(HD) ** -0.5
SCALE1 = float(C) ** -0.5
EPS0, EPS1 = 1e-5, 1e-6
LOWEST = -3.4028234e38

S_PRE = 4 + 2
S_PAIR = BLK + 2 + KT
S_POST = S_PRE + (PAIRS - 1) * S_PAIR + BLK + KT
S_BATCH = S_POST + KT + MT // 2 + MT
T_PAIR = 2 * BLK
T_POST = PAIRS * T_PAIR
T_BATCH = T_POST + 2 + 2 * MT
O_BATCH = 2 + 4 * PAIRS + 2 + NH * KT
O_GN1 = 2 + 4 * PAIRS
M_BATCH = PAIRS * BLK + MT
R_BATCH = 4 * PAIRS + NH
G_BATCH = 4 * PAIRS
E_QK = MT
E_K1 = E_QK + 4 * PAIRS
E_V1 = E_K1 + KT
E_BATCH = E_V1 + MT // 2
GN_STEPS = NH * KT + 4
assert S_BATCH % 2 == 0 and S_PAIR % 2 == 0 and S_POST % 2 == 0 and T_BATCH % 2 == 0 and O_BATCH % 2 == 0


def attention_blocks(nc, x, wq0, wk0, wv0, wp0, bq0, bk0, bv0, bp0, g0, be0,
                     wq1, wk1, wv1, wp1, bq1, bk1, bv1, bp1, g1, be1, ident, gmean, out):
    with ExitStack() as ctx:
        def sb(name, shape, dt=F32):
            return ctx.enter_context(nc.sbuf_tensor(name, shape, dt))

        def sem(name):
            return ctx.enter_context(nc.semaphore(name))

        def dram(name, shape):
            return nc.dram_tensor(name, shape, F32, kind="Internal").ap()

        WQK_D = dram("wqk_split", [PAIRS + 1, P, 2 * KT * 2 * P])
        WV_D = dram("wv_split", [P, 2 * KT * C])
        WP_D = dram("wp_split", [PAIRS, P, 2 * C])
        M1_D = dram("m1_split", [P, 2 * KT * C])
        M2_D = dram("m2_split", [P, 2 * KT * C])
        R_D = dram("inverse_sums", [2, GRP, P])

        xin = sb("xin", [P, KT, N])
        y = sb("y", [P, KT, N])
        xn = sb("xn", [P, 2, KT, N], F32R)
        kq = sb("kq", [P, 8, N], F32R)
        v = sb("v", [P, MT, 2 * C], F32R)
        pt = sb("pt", [P, 2 * MT * HALF], F32R)
        pr = sb("pr", [P, 2, N])
        vp = sb("vp", [P, MT, 4 * HD], F32R)
        wqk = sb("wqk", [P, 2, KT, 2 * P], F32R)
        wp = sb("wp", [P, 2, C], F32R)
        trow = sb("trow", [P, N])
        tw = sb("tw", [P, 2, KT, P], F32R)
        otmp = sb("otmp", [P, HALF])
        osum = sb("osum", [P, HALF])
        idn = sb("idn", [P, P])
        gm = sb("gm", [P, P])
        ones = sb("ones", [P, P])
        vec = sb("vec", [P, 14, KT])
        der = sb("der", [P, 4, KT])
        bb = sb("bb", [P, KT])
        t0 = sb("t0", [P, 1])
        bst = sb("bst", [P, KT, NH, 6])
        mv = sb("mv", [P, KT, 2])
        gs = sb("gs", [P, 8, KT])
        expo = sb("expo", [P, KT])
        nmax = sb("nmax", [P, 4])
        rmax = sb("rmax", [P, 4])
        pspare = sb("pspare", [P, 1])
        spare = sb("spare", [P, 8])
        rsum = sb("rsum", [P, 2, GRP])
        rinv = sb("rinv", [P, 2, GRP])
        rb = sb("rb", [P, 2, HALF])

        sps = [ctx.enter_context(nc.psum_tensor(f"sps{i}", [P, N], F32)) for i in range(2)]
        tps = [ctx.enter_context(nc.psum_tensor(f"tps{i}", [P, HALF], F32)) for i in range(2)]
        ops = [ctx.enter_context(nc.psum_tensor(f"ops{i}", [P, HALF], F32)) for i in range(2)]

        BQ0, BK0, BV0, BP0, G0, BE0, BQ1, BK1, BV1, BP1, G1, BE1 = range(12)
        KB1, TWC, BO0, BO1 = range(4)
        ptv = pt[:].rearrange("p (l m n) -> p l m n", l=2, m=MT)
        wbig = [pt[:, i * 2 * KT * C:(i + 1) * 2 * KT * C].rearrange("p (l k n) -> p l k n", l=2, k=KT)
                for i in range(2)]
        v0 = v[:].rearrange("p m (q x d) -> p m q x d", q=PAIRS, x=4)
        v1 = v[:].rearrange("p m (l c) -> p m l c", l=2)
        wqkf = wqk[:].rearrange("p l k n -> p (l k n)").bitcast(F32)
        wpf = wp[:].rearrange("p l n -> p (l n)").bitcast(F32)
        LOW, HIGH = slice(0, HD), slice(HD, P)
        own = (LOW, HIGH)
        other = (HIGH, LOW)

        s_ready = [sem("s_ready0"), sem("s_ready1")]
        s_free = [sem("s_free0"), sem("s_free1")]
        t_ready = [sem("t_ready0"), sem("t_ready1")]
        t_done = sem("t_done")
        hi_done = sem("hi_done")
        o_ready = [sem("o_ready0"), sem("o_ready1")]
        o_done = sem("o_done")
        raw_max = sem("raw_max")
        maxed = sem("maxed")
        inv_done = sem("inv_done")
        r_mid = sem("r_mid")
        r_in = sem("r_in")
        o_moved = sem("o_moved")
        o_mul = sem("o_mul")
        o_hi = sem("o_hi")
        o_split = sem("o_split")
        o_scaled = sem("o_scaled")
        ev_hi = sem("ev_hi")
        first_head = sem("first_head")
        first_tile = sem("first_tile")
        k_dup = sem("k_dup")
        vp_in = sem("vp_in")
        gn_step = sem("gn_step")
        gn_stat = sem("gn_stat")
        gn_pow = sem("gn_pow")
        gn_coef = sem("gn_coef")
        gn_val = sem("gn_val")
        gn_hi = sem("gn_hi")
        gn_lo = sem("gn_lo")
        x_in = sem("x_in")
        y_in = sem("y_in")
        wqk_in = sem("wqk_in")
        wp_in = sem("wp_in")
        wv_in = sem("wv_in")
        m_in = sem("m_in")
        y_out = sem("y_out")
        c_in = sem("c_in")
        p_in = sem("p_in")
        p_hi = sem("p_hi")
        p_lo = sem("p_lo")
        p_out = sem("p_out")
        p_mm = sem("p_mm")
        p_vec = sem("p_vec")
        p_one = sem("p_one")

        def s_unit(b, u):
            return u % 2, b * (S_BATCH // 2) + u // 2

        def s_pair(b, p, j):
            return j % 2, b * (S_BATCH // 2) + p * (S_PAIR // 2) + (S_PRE + j) // 2

        def o_unit(b, u):
            return u % 2, b * (O_BATCH // 2) + u // 2

        block = ctx.enter_context(nc.Block())
        stages = [(wq0,), (wk0,), (wv0,), (wp0,), (wk1, wq1), (wv1, wp1)]
        loaded = [16 * sum(len(w) for w in stages[:n + 1]) for n in range(len(stages))]
        stores = [2 * k for k in (PAIRS + 1, PAIRS + 1, 1, PAIRS, 1, 1)]
        stored = [16 * sum(stores[:n + 1]) for n in range(len(stages))]

        @block.sync
        def _(sp):
            for i, a in enumerate((bq0, bk0, bv0, bp0, g0, be0, bq1, bk1, bv1, bp1, g1, be1)):
                sp.dma_start(vec[:, i, :], a).then_inc(c_in, 16)
            sp.dma_start(idn[:], ident).then_inc(c_in, 16)
            sp.dma_start(gm[:], gmean).then_inc(c_in, 16)
            for n, weights in enumerate(stages):
                if n:
                    sp.wait_ge(p_lo, KT * n)
                if n == 4:
                    sp.wait_ge(p_mm, 1)
                for dst, w in zip((xin, y), weights):
                    sp.dma_start(dst[:, :, 0:C], w.rearrange("(k p) n -> p k n", p=P)).then_inc(p_in, 16)
                sp.wait_ge(p_lo, KT * (n + 1))
                for l in range(2):
                    src = xn[:, l, :, 0:C].bitcast(F32)
                    if n < 2:
                        for p in range(PAIRS + 1):
                            dst = WQK_D[p].rearrange("p (l k n) -> p l k n", l=2, k=KT)
                            q = p % PAIRS
                            sp.dma_start(dst[:, l, :, n * P:(n + 1) * P],
                                         src[:, :, q * P:(q + 1) * P]).then_inc(p_out, 16)
                    elif n == 3:
                        for p in range(PAIRS):
                            sp.dma_start(WP_D[p].rearrange("p (l n) -> p l n", l=2)[:, l, :],
                                         src[:, p, :]).then_inc(p_out, 16)
                    else:
                        dst = {2: WV_D, 4: M1_D, 5: M2_D}[n]
                        sp.dma_start(dst.rearrange("p (l k n) -> p l k n", l=2, k=KT)[:, l],
                                     src).then_inc(p_out, 16)
            sp.wait_ge(p_out, stored[-1])
            sp.dma_start(xin[:], x[0]).then_inc(x_in, 16)
            sp.dma_start(wqkf, WQK_D[0]).then_inc(wqk_in, 16)
            sp.dma_start(wpf, WP_D[0]).then_inc(wp_in, 16)
            sp.dma_start(pt[:, 0:2 * KT * C].bitcast(F32), WV_D).then_inc(wv_in, 16)

            sp.wait_ge(x_in, 16)
            sp.dma_start(y[:], xin[:]).then_inc(y_in, 16)

            def spread_inverse(c, slot):
                sp.wait_ge(inv_done, c + 1)
                sp.dma_start(R_D[slot].rearrange("g p -> p g"), rinv[:, slot, :],
                             allow_slow_non_contiguous=True).then_inc(r_mid, 16)
                sp.wait_ge(r_mid, 16 * (c + 1))
                src = R_D[slot].rearrange("g p -> (g p)").rearrange("(a n) -> a n", a=1)
                sp.dma_start(rb[:, slot, :], src.broadcast_to([P, HALF])).then_inc(r_in, 16)

            def after_qk(k_unit, q_unit, weights):
                sp.wait_ge(s_free[k_unit[0]], k_unit[1] + 2)
                for t in range(2, 6):
                    if t == 4:
                        sp.wait_ge(s_free[q_unit[0]], q_unit[1] + 2)
                    a, z = own[t % 2], other[t % 2]
                    sp.dma_start(kq[z, t, :].bitcast(F32), kq[a, t, :].bitcast(F32)).then_inc(k_dup, 16)
                sp.wait_ge(s_ready[q_unit[0]], q_unit[1] + 1)
                sp.dma_start(wqkf, weights).then_inc(wqk_in, 16)

            def load_vp(b, p):
                if not isinstance(p, int):
                    sp.wait_ge(o_ready[1], b * (O_BATCH // 2) + 2 * p + 1)
                sp.dma_start(vp[:].bitcast(F32), v[:, :, bass.ds(p * 4 * HD, 4 * HD)].bitcast(F32)).then_inc(vp_in, 16)

            with sp.Fori(0, B) as b:
                following = sp.snap((b + 1) % B)
                sp.wait_ge(y_in, b * 16 + 16)
                sp.wait_ge(gn_val, b * (2 * KT) + KT)
                sp.wait_ge(gn_hi, b * (2 * KT) + KT)
                sp.dma_start(xin[:], x[bass.ds(following, 1)].rearrange("b p k n -> (b p) k n")).then_inc(x_in, 16)

                v_unit = s_unit(b, 3)
                sp.wait_ge(s_free[v_unit[0]], v_unit[1] + 2)
                load_vp(b, 0)
                after_qk(s_unit(b, 4), s_unit(b, 5), WQK_D[1])
                with sp.Fori(0, PAIRS - 1) as p:
                    for g in range(4):
                        spread_inverse(b * R_BATCH + p * 4 + g, g % 2)
                    after_qk(s_pair(b, p, BLK), s_pair(b, p, BLK + 1), WQK_D[p + 2])
                    load_vp(b, p + 1)
                    proj = s_pair(b, p, BLK + 1 + KT)
                    sp.wait_ge(s_ready[proj[0]], proj[1] + 1)
                    sp.dma_start(wpf, WP_D[p + 1]).then_inc(wp_in, 16)
                for g in range(4):
                    spread_inverse(b * R_BATCH + 4 * (PAIRS - 1) + g, g % 2)
                pv = o_unit(b, O_GN1 - 1)
                sp.wait_ge(o_ready[pv[0]], pv[1] + 1)
                sp.dma_start(pt[:, 0:2 * KT * C].bitcast(F32), M1_D).then_inc(m_in, 16)
                sp.dma_start(pt[:, 2 * KT * C:].bitcast(F32), M2_D).then_inc(m_in, 16)
                proj = s_unit(b, S_POST - 1)
                sp.wait_ge(s_ready[proj[0]], proj[1] + 1)
                sp.dma_start(wpf, WP_D[0]).then_inc(wp_in, 16)
                for h in range(NH):
                    spread_inverse(b * R_BATCH + 4 * PAIRS + h, h)
                    for c in range(KT):
                        sp.wait_ge(o_done, b * O_BATCH + O_GN1 + 2 + h * KT + c + 3)
                        cols = slice(h * HALF, (h + 1) * HALF)
                        sp.dma_start(out[b, :, c, cols], y[:, c, cols]).then_inc(y_out, 16)
                pv = o_unit(b, O_BATCH - 1)
                sp.wait_ge(o_ready[pv[0]], pv[1] + 1)
                sp.dma_start(pt[:, 0:2 * KT * C].bitcast(F32), WV_D).then_inc(wv_in, 16)
                sp.wait_ge(x_in, b * 16 + 32)
                sp.wait_ge(y_out, b * (16 * KT * NH) + 16 * KT * NH)
                sp.dma_start(y[:], xin[:]).then_inc(y_in, 16)
            sp.wait_ge(y_in, 16 * (B + 1))
            sp.wait_ge(wv_in, 16 * (B + 1))
            sp.wait_ge(x_in, 16 * (B + 1))
            sp.wait_ge(wqk_in, 16 * (B * PAIRS + 1))
            sp.wait_ge(wp_in, 16 * (B * PAIRS + 1))

        @block.tensor
        def _(pe):
            mm = nc.tensor.matmul
            def by_vector(dst, w, col):
                for c in range(KT):
                    for k in range(KT):
                        ins = mm(dst[:, c:c + 1], w[:, k, c * P:(c + 1) * P], vec[:, col, k:k + 1],
                                 start=k == 0, stop=k == KT - 1)
                return ins

            def product():
                for c in range(KT):
                    for k in range(KT):
                        ins = mm(sps[c // 2][:, c % 2 * HALF:(c % 2 + 1) * HALF], xin[:, k, c * P:(c + 1) * P],
                                 y[:, k, 0:C], start=k == 0, stop=k == KT - 1)
                    ins.then_inc(p_mm, 1)

            pe.wait_ge(c_in, 16 * 14)
            pe.wait_ge(p_in, loaded[3])
            by_vector(ops[0], xin, BV0).then_inc(p_mm, 1)
            pe.wait_ge(p_in, loaded[4])
            pe.wait_ge(p_vec, 1)
            pe.wait_ge(p_one, 1)
            by_vector(ops[1][:, 0:KT], y, BK1)
            by_vector(ops[1][:, KT:2 * KT], xin, BQ1)
            for k in range(KT):
                last = mm(ops[1][:, 2 * KT:2 * KT + 1], ones[:], bb[:, k:k + 1], start=k == 0, stop=k == KT - 1)
            last.then_inc(p_mm, 1)
            product()
            pe.wait_ge(p_in, loaded[5])
            pe.wait_ge(p_lo, 5 * KT)
            pe.wait_ge(p_vec, 3)
            by_vector(ops[0], y, BV1).then_inc(p_mm, 1)
            product()
            pe.wait_ge(p_lo, 6 * KT)
            pe.wait_ge(p_vec, 7 + 2 * KT)

            def s_take(unit):
                pe.wait_ge(s_free[unit[0]], unit[1] + 1)
                return sps[unit[0]]

            def split_mm(dst, left, right):
                n = len(left)
                for k in range(n):
                    for i, (a, w) in enumerate(((0, 0), (0, 1), (1, 0))):
                        ins = mm(dst, left[k][a], right[k][w], start=k == 0 and i == 0,
                                 stop=k == n - 1 and i == 2)
                return ins

            def cut(t, lo, hi):
                return [[t[:, l, k, lo:hi] for l in range(2)] for k in range(KT)]

            def group_norm(b, u, which):
                for i in range(2):
                    bank, n = o_unit(b, u + i)
                    pe.wait_ge(o_done, b * O_BATCH + u + i + 1)
                    pe.wait_ge(gn_stat, b * (2 * (KT + 1)) + which * (KT + 1) + KT + i)
                    src = mv[:, :, 0] if i == 0 else gs[:, 1, :]
                    mm(ops[bank][:, 0:KT], gm[:], src, start=True, stop=True).then_inc(o_ready[bank], 1)

            def v_units(b, first, w):
                for m in range(0, MT, 2):
                    unit = s_unit(b, first + m // 2)
                    dst = s_take(unit)
                    for j in range(2):
                        last = split_mm(dst[:, j * HALF:(j + 1) * HALF], cut(xn, (m + j) * P, (m + j + 1) * P),
                                        cut(w, 0, C))
                    last.then_inc(s_ready[unit[0]], 1)

            def channel_unit(unit, w, lo):
                dst = s_take(unit)
                for h in range(NH):
                    last = split_mm(dst[:, h * HALF:(h + 1) * HALF], cut(w, lo, lo + P),
                                    cut(xn, h * HALF, (h + 1) * HALF))
                last.then_inc(s_ready[unit[0]], 1)

            def scores0(unit, i):
                head, m = i // MT, i % MT
                dst = s_take(unit)
                for h in range(NH):
                    for l in range(2):
                        last = mm(dst[:, h * HALF:(h + 1) * HALF], kq[:, head, m * P:(m + 1) * P],
                                  kq[:, 2 + 2 * l + head, h * HALF:(h + 1) * HALF], start=l == 0, stop=l == 1)
                last.then_inc(s_ready[unit[0]], 1)

            def transposes(t, unit, i):
                pe.wait_ge(s_free[unit[0]], unit[1] + 2)
                for h in range(2):
                    pe.wait_ge(t_done, t + h + 1)
                    for j in range(4):
                        last = nc.tensor.transpose(tps[h][:, j * P:(j + 1) * P],
                                                   pr[:, i % 2, (4 * h + j) * P:(4 * h + j + 1) * P], idn[:])
                    last.then_inc(t_ready[h], 1)

            def pv0(b, p, g):
                pe.wait_ge(o_done, b * O_BATCH + p * 4 + 2 + g + 1)
                pe.wait_ge(t_done, b * T_BATCH + p * T_PAIR + 2 * GRP * (g + 1) + 2)
                head = g // 2
                for m in range(MT):
                    for l in range(2):
                        last = mm(ops[g % 2][:], vp[:, m, head * P:(head + 1) * P], ptv[:, l, m, :],
                                  start=m == 0 and l == 0, stop=m == MT - 1 and l == 1)
                last.then_inc(o_ready[g % 2], 1)

            def pair(b, p, unit_of, more):
                pe.wait_ge(k_dup, b * (64 * PAIRS) + p * 64 + 64)
                pe.wait_ge(vp_in, b * (16 * PAIRS) + p * 16 + 16)
                scores0(unit_of(0), 0)
                scores0(unit_of(1), 1)
                for i in range(BLK):
                    if i + 2 < BLK:
                        scores0(unit_of(i + 2), i + 2)
                    if i and i % GRP == 0:
                        pv0(b, p, i // GRP - 1)
                    transposes(b * T_BATCH + p * T_PAIR + 2 * i, unit_of(i), i)
                if more:
                    pe.wait_ge(wqk_in, b * (16 * PAIRS) + p * 16 + 32)
                    channel_unit(unit_of(BLK), wqk, P)
                pv0(b, p, 3)
                if more:
                    channel_unit(unit_of(BLK + 1), wqk, 0)
                pe.wait_ge(wp_in, b * (16 * PAIRS) + p * 16 + 16)
                pe.wait_ge(o_split, b * G_BATCH + p * 4 + 5)
                for c in range(KT):
                    unit = unit_of(BLK + (2 if more else 0) + c)
                    dst = s_take(unit)
                    for h in range(NH):
                        last = split_mm(dst[:, h * HALF:(h + 1) * HALF],
                                        [[wp[:, l, c * P:(c + 1) * P] for l in range(2)]],
                                        [[kq[:, 6 + l, h * HALF:(h + 1) * HALF] for l in range(2)]])
                    last.then_inc(s_ready[unit[0]], 1)

            with pe.Fori(0, B) as b:
                group_norm(b, 0, 0)
                pe.wait_ge(gn_lo, b * (2 * KT) + KT)
                pe.wait_ge(wv_in, b * 16 + 16)
                v_units(b, 0, wbig[0])
                pe.wait_ge(wqk_in, b * (16 * PAIRS) + 16)
                channel_unit(s_unit(b, 4), wqk, P)
                channel_unit(s_unit(b, 5), wqk, 0)
                with pe.Fori(0, PAIRS - 1) as p:
                    pair(b, p, lambda j: s_pair(b, p, j), True)
                pair(b, PAIRS - 1, lambda j: s_unit(b, S_PRE + (PAIRS - 1) * S_PAIR + j), False)

                group_norm(b, O_GN1, 1)
                pe.wait_ge(gn_lo, b * (2 * KT) + 2 * KT)
                pe.wait_ge(m_in, b * 32 + 32)
                for c in range(KT):
                    channel_unit(s_unit(b, S_POST + c), wbig[0], c * P)
                for h in range(NH):
                    pe.wait_ge(t_done, b * T_BATCH + T_POST + h + 1)
                    split_mm(tps[h][:], cut(tw, 0, P), cut(xn, h * HALF, (h + 1) * HALF)).then_inc(t_ready[h], 1)
                v_units(b, S_POST + KT, wbig[1])

                def scores1(i):
                    unit = s_unit(b, S_POST + KT + MT // 2 + i)
                    dst = s_take(unit)
                    for h in range(NH):
                        last = split_mm(dst[:, h * HALF:(h + 1) * HALF], cut(xn, i * P, (i + 1) * P),
                                        [[kq[:, l * KT + k, h * HALF:(h + 1) * HALF] for l in range(2)]
                                         for k in range(KT)])
                    last.then_inc(s_ready[unit[0]], 1)

                def pv1(h):
                    pe.wait_ge(t_done, b * T_BATCH + T_POST + 2 + 2 * GRP * (h + 1) + 2)
                    for c in range(KT):
                        o = O_GN1 + 2 + h * KT + c
                        pe.wait_ge(o_done, b * O_BATCH + o + 1)
                        split_mm(ops[o % 2][:],
                                 [[v1[:, m, l, c * P:(c + 1) * P] for l in range(2)] for m in range(MT)],
                                 [[ptv[:, l, m, :] for l in range(2)] for m in range(MT)]).then_inc(o_ready[o % 2], 1)

                scores1(0)
                scores1(1)
                for i in range(MT):
                    if i + 2 < MT:
                        scores1(i + 2)
                    if i == GRP:
                        pv1(0)
                    transposes(b * T_BATCH + T_POST + 2 + 2 * i, s_unit(b, S_POST + KT + MT // 2 + i), i)
                pv1(1)

        @block.scalar
        def _(act):
            def hi_of(dst, src, bias, sem, scale=1.0):
                nc.scalar.activation(dst, src, ACT.Identity, bias=bias, scale=scale).then_inc(sem, 1)

            def group_norm(b, src, which):
                act.wait_ge(gn_coef, b * 2 + which + 1)
                for k in range(KT):
                    hi_of(xn[:, 0, k, :], src[:, k, :], gs[:, 3, k:k + 1], gn_hi, gs[:, 6, k:k + 1])

            def filled(unit):
                act.wait_ge(s_ready[unit[0]], unit[1] + 1)
                return sps[unit[0]]

            def exp(i, m, unit, free):
                act.wait_ge(maxed, m + 1)
                if free is not None:
                    act.wait_ge(t_ready[1], free)
                nc.scalar.activation(pr[:, i % 2, :], sps[unit[0]][:], ACT.Exp, bias=nmax[:, i % 4:i % 4 + 1],
                                     accum_out=rsum[:, i // GRP % 2, i % GRP:i % GRP + 1]).then_inc(s_free[unit[0]], 1)

            def p_hi(t, m, i):
                for h in range(2):
                    act.wait_ge(t_ready[h], t + 1)
                    dst = ptv[:, 0, 4 * h:4 * h + 4, i % GRP * P:(i % GRP + 1) * P]
                    nc.scalar.activation(dst, tps[h][:].rearrange("p (m n) -> p m n", m=4),
                                         ACT.Identity, bias=0.0).then_inc(hi_done, 1)

            def move(b, p, g):
                e = g // 2
                act.wait_ge(o_ready[g % 2], b * (O_BATCH // 2) + p * 2 + 1 + g // 2 + 1)
                act.wait_ge(o_done, b * O_BATCH + p * 4 + 2 + g + 2)
                nc.scalar.activation(otmp[own[e], :], ops[g % 2][other[e], :], ACT.Identity,
                                     bias=0.0).then_inc(o_moved, 1)

            def pair(b, p, unit_of, more):
                tn = b * (T_BATCH // 2) + p * BLK
                m = b * M_BATCH + p * BLK
                exp(0, m, unit_of(0), None)
                exp(1, m + 1, unit_of(1), None)
                for i in range(BLK):
                    if i % GRP == 0:
                        g = (i // GRP - 1) % 4
                        act.wait_ge(o_ready[g % 2], b * (O_BATCH // 2) + p * 2 + (1 + g // 2 + 1 if i else 1))
                    p_hi(tn + i, m + i, i)
                    if i + 2 < BLK:
                        exp(i + 2, m + i + 2, unit_of(i + 2), tn + i + 1)
                    if i and i % GRP == 0:
                        move(b, p, i // GRP - 1)
                if more:
                    src = filled(unit_of(BLK))
                    for e in range(2):
                        hi_of(kq[own[e], 2 + e, :], src[own[e], :], vec[own[e], BK0, bass.ds(p + 1, 1)], ev_hi)
                move(b, p, 3)
                if more:
                    src = filled(unit_of(BLK + 1))
                    for e in range(2):
                        hi_of(kq[own[e], e, :], src[own[e], :], vec[own[e], BQ0, bass.ds(p + 1, 1)], ev_hi)

            with act.Fori(0, B) as b:
                act.wait_ge(x_in, b * 16 + 16)
                group_norm(b, xin, 0)
                for u in range(MT // 2):
                    src = filled(s_unit(b, u))
                    for j in range(2):
                        nc.scalar.activation(v0[:, 2 * u + j, :, 0::3, :],
                                             src[:, j * HALF:(j + 1) * HALF].rearrange("p (q e d) -> p q e d", q=PAIRS, e=2),
                                             ACT.Identity, bias=0.0).then_inc(ev_hi, 1)
                for j, (slot, col) in enumerate(((2, BK0), (0, BQ0))):
                    src = filled(s_unit(b, 4 + j))
                    for e in range(2):
                        hi_of(kq[own[e], slot + e, :], src[own[e], :], vec[own[e], col, 0:1], ev_hi)
                with act.Fori(0, PAIRS - 1) as p:
                    pair(b, p, lambda j: s_pair(b, p, j), True)
                pair(b, PAIRS - 1, lambda j: s_unit(b, S_PRE + (PAIRS - 1) * S_PAIR + j), False)

                group_norm(b, y, 1)
                for c in range(KT):
                    hi_of(kq[:, c, :], filled(s_unit(b, S_POST + c))[:], der[:, KB1, c:c + 1], ev_hi)
                for u in range(MT // 2):
                    src = filled(s_unit(b, S_POST + KT + u))
                    nc.scalar.activation(v1[:, 2 * u:2 * u + 2, 0, :], src[:].rearrange("p (m c) -> p m c", m=2),
                                         ACT.Identity, bias=0.0).then_inc(ev_hi, 1)
                first = S_POST + KT + MT // 2
                tn = b * (T_BATCH // 2) + T_POST // 2 + 1
                m = b * M_BATCH + PAIRS * BLK
                exp(0, m, s_unit(b, first), None)
                exp(1, m + 1, s_unit(b, first + 1), None)
                for i in range(MT):
                    if i == GRP:
                        o = O_GN1 + 2 + KT - 1
                        act.wait_ge(o_ready[o % 2], b * (O_BATCH // 2) + o // 2 + 1)
                    p_hi(tn + i, m + i, i)
                    if i + 2 < MT:
                        exp(i + 2, m + i + 2, s_unit(b, first + i + 2), tn + i + 1)

        @block.vector
        def _(dve):
            op = nc.vector
            op.memset(ones[:], 1.0).then_inc(p_one, 1)
            op.memset(expo[:], -0.5).then_inc(p_one, 1)
            for n, s in enumerate((s_free[0], s_free[1], t_done, t_done, o_done, o_done)):
                op.memset(spare[:, n:n + 1], 0.0).then_inc(s, 1)
            dve.wait_ge(c_in, 16 * 14)
            dve.wait_ge(p_one, 2)
            op.tensor_tensor(bb[:], vec[:, BQ1, :], vec[:, BK1, :], ALU.mult).then_inc(p_vec, 1)
            op.tensor_scalar(vec[:, BQ0, :], vec[:, BQ0, :], SCALE0, None, ALU.mult).then_inc(p_vec, 1)

            for n in range(len(stages)):
                dve.wait_ge(p_in, loaded[n])
                if n:
                    dve.wait_ge(p_out, stored[n - 1])
                scale = {0: SCALE0, 4: SCALE1}.get(n, 1.0)
                if n == 4:
                    dve.wait_ge(p_mm, 1)
                    op.tensor_tensor(der[:, BO0, :], ops[0][:, 0:KT], vec[:, BP0, :], ALU.add).then_inc(p_vec, 1)
                    dve.wait_ge(p_mm, 2)
                    op.tensor_scalar(der[:, KB1, :], ops[1][:, 0:KT], SCALE1, None, ALU.mult).then_inc(p_vec, 1)
                    op.tensor_scalar(der[:, TWC, :], ops[1][:, KT:2 * KT], SCALE1, None, ALU.mult).then_inc(p_vec, 1)
                    op.tensor_scalar(t0[:], ops[1][:, 2 * KT:2 * KT + 1], SCALE1, None, ALU.mult).then_inc(p_vec, 1)
                    dve.wait_ge(p_vec, 6)
                    for k in range(KT):
                        op.tensor_scalar(tw[:, 0, k, :], ones[:], der[:, TWC, k:k + 1], None, ALU.mult).then_inc(p_vec, 1)
                    dve.wait_ge(p_vec, 6 + KT)
                    for k in range(KT):
                        op.scalar_tensor_tensor(out=tw[:, 1, k, :], in0=ones[:], scalar=der[:, TWC, k:k + 1],
                                                in1=tw[:, 0, k, :].bitcast(F32), op0=ALU.mult,
                                                op1=ALU.subtract).then_inc(p_vec, 1)
                if n == 5:
                    dve.wait_ge(p_mm, 2 + KT + 1)
                    op.tensor_tensor(der[:, BO1, :], ops[0][:, 0:KT], vec[:, BP1, :], ALU.add).then_inc(p_vec, 1)
                for k in range(KT):
                    if n < 4:
                        src = xin[:, k, 0:C]
                    else:
                        dve.wait_ge(p_mm, (2 if n == 4 else 3 + KT) + k + 1)
                        src = sps[k // 2][:, k % 2 * HALF:(k % 2 + 1) * HALF]
                    op.tensor_scalar(xn[:, 0, k, 0:C], src, scale, None, ALU.mult).then_inc(p_hi, 1)
                    dve.wait_ge(p_hi, KT * n + k + 1)
                    op.scalar_tensor_tensor(out=xn[:, 1, k, 0:C], in0=src, scalar=scale,
                                            in1=xn[:, 0, k, 0:C].bitcast(F32), op0=ALU.mult,
                                            op1=ALU.subtract).then_inc(p_lo, 1)
            dve.wait_ge(p_vec, 7 + 2 * KT)
            dve.wait_ge(p_out, stored[-1])

            def filled(unit):
                dve.wait_ge(s_ready[unit[0]], unit[1] + 1)
                return sps[unit[0]]

            def group_norm(b, src, u, which, eps, gamma, beta):
                step0 = b * (2 * GN_STEPS) + which * GN_STEPS
                stat0 = b * (2 * (KT + 1)) + which * (KT + 1)
                for k in range(KT):
                    for h in range(NH):
                        op.bn_stats(bst[:, k, h, :], src[:, k, h * HALF:(h + 1) * HALF]).then_inc(gn_step, 1)
                dve.wait_ge(gn_step, step0 + 8)
                op.memset(spare[:, 6:7], 0.0)
                for k in range(KT):
                    op.bn_aggr(mv[:, k, :], bst[:, k, :, :].rearrange("p h s -> p (h s)")).then_inc(gn_stat, 1)
                dve.wait_ge(gn_stat, stat0 + KT)
                bank, n = o_unit(b, u)
                dve.wait_ge(o_ready[bank], n + 1)
                op.tensor_tensor(gs[:, 0, :], mv[:, :, 0], ops[bank][:, 0:KT], ALU.subtract).then_inc(gn_step, 1)
                op.tensor_copy(gs[:, 2, :], ops[bank][:, 0:KT]).then_inc(o_done, 1)
                dve.wait_ge(gn_step, step0 + 9)
                op.tensor_tensor(gs[:, 4, :], gs[:, 0, :], gs[:, 0, :], ALU.mult).then_inc(gn_step, 1)
                dve.wait_ge(gn_step, step0 + 10)
                op.tensor_tensor(gs[:, 1, :], gs[:, 4, :], mv[:, :, 1], ALU.add).then_inc(gn_stat, 1)
                bank, n = o_unit(b, u + 1)
                dve.wait_ge(o_ready[bank], n + 1)
                op.tensor_scalar(gs[:, 5, :], ops[bank][:, 0:KT], eps, None, ALU.add).then_inc(o_done, 1)
                dve.wait_ge(gn_pow, b * 2 + which + 1)
                op.tensor_tensor(gs[:, 6, :], gs[:, 7, :], vec[:, gamma, :], ALU.mult).then_inc(gn_step, 1)
                dve.wait_ge(gn_step, step0 + 11)
                dve.wait_ge(o_done, b * O_BATCH + u + 2 + 2)
                op.tensor_tensor(gs[:, 4, :], gs[:, 2, :], gs[:, 6, :], ALU.mult).then_inc(gn_step, 1)
                dve.wait_ge(gn_step, step0 + 12)
                op.tensor_tensor(gs[:, 3, :], vec[:, beta, :], gs[:, 4, :], ALU.subtract).then_inc(gn_coef, 1)
                dve.wait_ge(gn_coef, b * 2 + which + 1)
                for k in range(KT):
                    if k >= 2:
                        dve.wait_ge(gn_lo, b * (2 * KT) + which * KT + k - 1)
                    op.tensor_scalar(pr[:, k % 2, :], src[:, k, :], gs[:, 6, k:k + 1], gs[:, 3, k:k + 1],
                                     ALU.mult, ALU.add).then_inc(gn_val, 1)
                    dve.wait_ge(gn_val, b * (2 * KT) + which * KT + k + 1)
                    dve.wait_ge(gn_hi, b * (2 * KT) + which * KT + k + 1)
                    op.tensor_tensor(xn[:, 1, k, :], pr[:, k % 2, :], xn[:, 0, k, :].bitcast(F32),
                                     ALU.subtract).then_inc(gn_lo, 1)

            def lo_of(dst, src, bias, hi, sem):
                op.scalar_tensor_tensor(out=dst, in0=src, scalar=bias, in1=hi.bitcast(F32), op0=ALU.add,
                                        op1=ALU.subtract).then_inc(sem, 1)

            def k_lo(unit, e0, bias):
                src = filled(unit)
                for e in range(2):
                    dve.wait_ge(ev_hi, e0 + e + 1)
                    lo_of(kq[own[e], 4 + e, :], src[own[e], :], bias(BK0, e), kq[own[e], 2 + e, :],
                          s_free[unit[0]] if e else first_head)

            def q_lo(unit, e0, bias):
                src = filled(unit)
                for e in range(2):
                    dve.wait_ge(ev_hi, e0 + 2 + e + 1)
                    lo_of(kq[other[e], e, :], src[own[e], :], bias(BQ0, e), kq[own[e], e, :],
                          s_free[unit[0]] if e else first_head)

            def row_max(unit, m, i):
                src = filled(unit)
                op.tensor_reduce(out=nmax[:, i % 4:i % 4 + 1], in_=src[:], axis=AX.X, op=ALU.max,
                                 negate=True).then_inc(maxed, 1)

            def p_lo_part(m, i):
                for h in range(2):
                    dve.wait_ge(hi_done, m * 2 + h + 1)
                    cols = slice(i % GRP * P, (i % GRP + 1) * P)
                    op.tensor_tensor(ptv[:, 1, 4 * h:4 * h + 4, cols], tps[h][:].rearrange("p (m n) -> p m n", m=4),
                                     ptv[:, 0, 4 * h:4 * h + 4, cols].bitcast(F32), ALU.subtract).then_inc(t_done, 1)

            def inverse(unit, i):
                dve.wait_ge(s_free[unit[0]], unit[1] + 2)
                slot = i // GRP % 2
                op.reciprocal(rinv[:, slot, :], rsum[:, slot, :]).then_inc(inv_done, 1)

            def joined(b, p, g):
                e = g // 2
                c = b * G_BATCH + p * 4 + g
                dve.wait_ge(o_moved, c + 1)
                dve.wait_ge(o_split, c + 1)
                op.tensor_tensor(osum[own[e], :], ops[g % 2][own[e], :], otmp[own[e], :], ALU.add).then_inc(o_done, 1)

            def pair(b, p, unit_of, more):
                m = b * M_BATCH + p * BLK
                row_max(unit_of(0), m, 0)
                row_max(unit_of(1), m + 1, 1)
                for i in range(BLK):
                    if i + 2 < BLK:
                        row_max(unit_of(i + 2), m + i + 2, i + 2)
                    if i > 1 and i % GRP == 1:
                        joined(b, p, i // GRP - 1)
                    if i % GRP == GRP - 1:
                        inverse(unit_of(i), i)
                    p_lo_part(m + i, i)
                if more:
                    e0 = b * E_BATCH + p * 4 + (E_QK + 4)
                    k_lo(unit_of(BLK), e0, lambda col, e: vec[own[e], col, bass.ds(p + 1, 1)])
                joined(b, p, 3)
                if more:
                    q_lo(unit_of(BLK + 1), e0, lambda col, e: vec[own[e], col, bass.ds(p + 1, 1)])
                dve.wait_ge(y_in, b * 16 + 16)
                for c in range(KT):
                    unit = unit_of(BLK + (2 if more else 0) + c)
                    src = filled(unit)
                    if more:
                        op.tensor_tensor(y[:, c, :], src[:], y[:, c, :], ALU.add).then_inc(s_free[unit[0]], 1)
                    else:
                        op.scalar_tensor_tensor(out=y[:, c, :], in0=src[:], scalar=der[:, BO0, c:c + 1],
                                                in1=y[:, c, :], op0=ALU.add, op1=ALU.add).then_inc(s_free[unit[0]], 1)

            with dve.Fori(0, B) as b:
                dve.wait_ge(x_in, b * 16 + 16)
                group_norm(b, xin, 0, 0, EPS0, G0, BE0)
                for u in range(MT // 2):
                    unit = s_unit(b, u)
                    src = filled(unit)
                    for j in range(2):
                        dve.wait_ge(ev_hi, b * E_BATCH + 2 * u + j + 1)
                        w = v0[:, 2 * u + j]
                        op.tensor_tensor(w[:, :, 1:3, :],
                                         src[:, j * HALF:(j + 1) * HALF].rearrange("p (q e d) -> p q e d", q=PAIRS, e=2),
                                         w[:, :, 0::3, :].bitcast(F32), ALU.subtract).then_inc(
                                             s_free[unit[0]] if j else first_tile, 1)
                first = lambda col, e: vec[own[e], col, 0:1]
                k_lo(s_unit(b, 4), b * E_BATCH + E_QK, first)
                q_lo(s_unit(b, 5), b * E_BATCH + E_QK, first)
                with dve.Fori(0, PAIRS - 1) as p:
                    pair(b, p, lambda j: s_pair(b, p, j), True)
                pair(b, PAIRS - 1, lambda j: s_unit(b, S_PRE + (PAIRS - 1) * S_PAIR + j), False)
                for j in (S_POST - 2, S_POST - 1):
                    unit = s_unit(b, j)
                    dve.wait_ge(s_free[unit[0]], unit[1] + 2)

                group_norm(b, y, O_GN1, 1, EPS1, G1, BE1)
                for c in range(KT):
                    unit = s_unit(b, S_POST + c)
                    src = filled(unit)
                    dve.wait_ge(ev_hi, b * E_BATCH + E_K1 + c + 1)
                    lo_of(kq[:, KT + c, :], src[:], der[:, KB1, c:c + 1], kq[:, c, :], s_free[unit[0]])
                for h in range(NH):
                    dve.wait_ge(t_ready[h], b * (T_BATCH // 2) + T_POST // 2 + 1)
                    op.tensor_scalar(trow[:, h * HALF:(h + 1) * HALF], tps[h][:], t0[:], None, ALU.add).then_inc(t_done, 1)
                for u in range(MT // 2):
                    unit = s_unit(b, S_POST + KT + u)
                    src = filled(unit)
                    dve.wait_ge(ev_hi, b * E_BATCH + E_V1 + u + 1)
                    op.tensor_tensor(v1[:, 2 * u:2 * u + 2, 1, :], src[:].rearrange("p (m c) -> p m c", m=2),
                                     v1[:, 2 * u:2 * u + 2, 0, :].bitcast(F32), ALU.subtract).then_inc(s_free[unit[0]], 1)
                dve.wait_ge(t_done, b * T_BATCH + T_POST + 2 + 2)
                m = b * M_BATCH + PAIRS * BLK

                def row_max1(i):
                    unit = s_unit(b, S_POST + KT + MT // 2 + i)
                    src = filled(unit)
                    op.memset(spare[:, 7:8], 0.0)
                    op.tensor_tensor_reduce(out=src[:], in0=src[:], in1=trow[:], scale=1.0, scalar=LOWEST,
                                            op0=ALU.add, op1=ALU.max,
                                            accum_out=rmax[:, i % 4:i % 4 + 1]).then_inc(raw_max, 1)
                    dve.wait_ge(raw_max, b * MT + i + 1)
                    op.tensor_scalar(nmax[:, i % 4:i % 4 + 1], rmax[:, i % 4:i % 4 + 1], -1.0, None,
                                     ALU.mult).then_inc(maxed, 1)

                def residual(h):
                    dve.wait_ge(r_in, b * (16 * R_BATCH) + 16 * (4 * PAIRS + h + 1))
                    for c in range(KT):
                        o = O_GN1 + 2 + h * KT + c
                        k = b * (NH * KT) + h * KT + c
                        cols = slice(h * HALF, (h + 1) * HALF)
                        dve.wait_ge(o_ready[o % 2], b * (O_BATCH // 2) + o // 2 + 1)
                        op.tensor_tensor(osum[:], ops[o % 2][:], rb[:, h, :], ALU.mult).then_inc(o_scaled, 1)
                        dve.wait_ge(o_scaled, k + 1)
                        op.scalar_tensor_tensor(out=y[:, c, cols], in0=osum[:], scalar=der[:, BO1, c:c + 1],
                                                in1=y[:, c, cols], op0=ALU.add, op1=ALU.add).then_inc(o_done, 1)
                        dve.wait_ge(o_done, b * O_BATCH + o + 3)

                row_max1(0)
                row_max1(1)
                for i in range(MT):
                    if i + 2 < MT:
                        row_max1(i + 2)
                    if i == GRP:
                        residual(0)
                    if i % GRP == GRP - 1:
                        inverse(s_unit(b, S_POST + KT + MT // 2 + i), i)
                    p_lo_part(m + i, i)
                residual(1)

        @block.gpsimd
        def _(pool):
            op = nc.gpsimd

            def group_norm(b, u, which):
                pool.wait_ge(o_done, b * O_BATCH + u + 2 + 2)
                op.tensor_tensor(gs[:, 7, :], gs[:, 5, :], expo[:], ALU.pow).then_inc(gn_pow, 1)

            def pair(b, p):
                for g in range(4):
                    c = b * G_BATCH + p * 4 + g
                    w = own[g // 2]
                    cols = slice(g % 2 * HALF, (g % 2 + 1) * HALF)
                    pool.wait_ge(o_done, b * O_BATCH + p * 4 + 2 + g + 3)
                    pool.wait_ge(r_in, b * (16 * R_BATCH) + p * 64 + 16 * (g + 1))
                    op.tensor_tensor(kq[w, 6, cols], osum[w, :], rb[w, g % 2, :], ALU.mult).then_inc(o_hi, 1)
                    pool.wait_ge(o_hi, c + 1)
                    op.tensor_tensor(osum[w, :], osum[w, :], rb[w, g % 2, :], ALU.mult).then_inc(o_mul, 1)
                    pool.wait_ge(o_mul, c + 1)
                    op.tensor_tensor(kq[w, 7, cols], osum[w, :], kq[w, 6, cols].bitcast(F32),
                                     ALU.subtract).then_inc(o_split, 1)

            pool.wait_ge(p_one, 2)
            op.memset(pspare[:], 0.0).then_inc(o_split, 1)
            with pool.Fori(0, B) as b:
                group_norm(b, 0, 0)
                with pool.Fori(0, PAIRS) as p:
                    pair(b, p)
                group_norm(b, O_GN1, 1)

    return nc


def kernel(**inputs):
    import numpy as _np
    import concourse.bacc as _bacc
    from concourse import mybir as _mybir
    from concourse.bass_utils import run_bass_kernel_spmd as _run

    def arr(name):
        return _np.asarray(inputs[name])

    def column(a):
        return _np.ascontiguousarray(a.reshape(-1, P).T)

    wqkv, bqkv = arr("L0_conv_w_qkv"), arr("L0_conv_b_qkv")
    xl = arr("x").reshape(B, KT, P, N).transpose(0, 2, 1, 3)
    gmean = _np.kron(_np.eye(P * GROUPS // C), _np.full((C // GROUPS,) * 2, GROUPS / C)).astype(_np.float32)
    given = dict(
        x=xl, wq0=wqkv[0:C].T, wk0=wqkv[C:2 * C].T, wv0=wqkv[2 * C:].T, wp0=arr("L0_conv_w_proj").T,
        bq0=column(bqkv[0:C]), bk0=column(bqkv[C:2 * C]), bv0=column(bqkv[2 * C:]),
        bp0=column(arr("L0_conv_b_proj")), g0=column(arr("L0_conv_gamma")), be0=column(arr("L0_conv_beta")),
        wq1=arr("L1_conv_q_w"), wk1=arr("L1_conv_k_w"), wv1=arr("L1_conv_v_w"), wp1=arr("L1_conv_proj_w").T,
        bq1=column(arr("L1_conv_q_b")), bk1=column(arr("L1_conv_k_b")), bv1=column(arr("L1_conv_v_b")),
        bp1=column(arr("L1_conv_proj_b")), g1=column(arr("L1_conv_gn_gamma")), be1=column(arr("L1_conv_gn_beta")),
        ident=_np.eye(P, dtype=_np.float32), gmean=gmean)
    nc = _bacc.Bacc("TRN2", target_bir_lowering=False, num_devices=1)
    arrays, args = {}, {}
    for name, a in given.items():
        a = _np.ascontiguousarray(a)
        arrays[f"in_{name}"] = a
        args[name] = nc.dram_tensor(f"in_{name}", a.shape, _mybir.dt.from_np(a.dtype), kind="ExternalInput").ap()
    args["out"] = nc.dram_tensor("out_x", (B, P, KT, N), _mybir.dt.float32, kind="ExternalOutput").ap()
    attention_blocks(nc, **args)
    r = _run(nc, [arrays], core_ids=[0])
    got = r.results[0]["out_x"]
    return _np.ascontiguousarray(got.transpose(0, 2, 1, 3)).reshape(B, C, 32, 32)
```

```python
from contextlib import ExitStack

import concourse.bass as bass
from concourse import mybir

ALU = mybir.AluOpType
ACT = mybir.ActivationFunctionType
AX = mybir.AxisListType
F32 = mybir.dt.float32
F32R = mybir.dt.float32r

P = 128
B, C, N = 8, 512, 1024
HEADS, GROUPS = 8, 32
HD = C // HEADS
KT = C // P
MT = N // P
HALF = 512
NH = N // HALF
PAIRS = HEADS // 2
BLK = 2 * MT
GRP = HALF // P
SCALE0 = float(HD) ** -0.5
SCALE1 = float(C) ** -0.5
EPS0, EPS1 = 1e-5, 1e-6
LOWEST = -3.4028234e38

S_PRE = 2 + MT // 2
S_PAIR = BLK + 2 + KT
S_POST = S_PRE + (PAIRS - 1) * S_PAIR + BLK + KT
S_BATCH = S_POST + KT + MT // 2 + MT
T_PAIR = 2 * BLK
T_POST = PAIRS * T_PAIR
T_BATCH = T_POST + 2 + 2 * MT
O_GN1 = 4 * PAIRS
O_GN0 = O_GN1 + 2
O_PV1 = O_GN0 + 2
O_BATCH = O_PV1 + NH * KT
M_BATCH = PAIRS * BLK + MT
R_BATCH = 4 * PAIRS + NH
G_BATCH = 4 * PAIRS
E_PAIR = 5
E_K1 = 4 + (PAIRS - 1) * E_PAIR + 1
E_V1 = E_K1 + KT
E_BATCH = E_V1 + MT // 2
GN_STEPS = NH * KT + 4
assert S_BATCH % 2 == 0 and S_PAIR % 2 == 0 and S_POST % 2 == 0 and T_BATCH % 2 == 0 and O_BATCH % 2 == 0


def attention_blocks(nc, x, wq0, wk0, wv0, wp0, bq0, bk0, bv0, bp0, g0, be0,
                     wq1, wk1, wv1, wp1, bq1, bk1, bv1, bp1, g1, be1, ident, gmean, out):
    with ExitStack() as ctx:
        def sb(name, shape, dt=F32):
            return ctx.enter_context(nc.sbuf_tensor(name, shape, dt))

        def sem(name):
            return ctx.enter_context(nc.semaphore(name))

        def dram(name, shape):
            return nc.dram_tensor(name, shape, F32, kind="Internal").ap()

        WQK_D = dram("wqk_split", [PAIRS + 1, P, 2 * KT * 2 * P])
        WV_D = dram("wv_split", [P, 2 * KT * C])
        WP_D = dram("wp_split", [PAIRS, P, 2 * C])
        M1_D = dram("m1_split", [P, 2 * KT * C])
        M2_D = dram("m2_split", [P, 2 * KT * C])
        R_D = dram("inverse_sums", [2, GRP, P])

        base = (nc.sbuf_base + 31) // 32 * 32
        sb("arena", [P, 3 * KT * N])

        def at(name, shape, k, dt=F32):
            return nc.alloc_sbuf_tensor_at(name, shape, dt, offset=base + 4 * k)

        xin = at("xin", [P, KT, N], 0)
        pb_hi = at("pb_hi", [P, MT, HALF], 0, F32R)
        v = at("v", [P, MT, 2 * C], KT * N, F32R)
        v32 = at("v32", [P, MT, C], KT * N)
        pb_lo = at("pb_lo", [P, MT, HALF], 2 * KT * N, F32R)
        y = sb("y", [P, KT, N])
        xn = sb("xn", [P, 2, KT, N], F32R)
        kq = sb("kq", [P, 8, N], F32R)
        pt = sb("pt", [P, 2 * MT * HALF], F32R)
        pr = sb("pr", [P, 2, N])
        vp = sb("vp", [P, MT, 4 * HD], F32R)
        wqk = sb("wqk", [P, 2, KT, 2 * P], F32R)
        wp = sb("wp", [P, 2, C], F32R)
        trow = sb("trow", [P, N])
        tw = sb("tw", [P, 2, KT, P], F32R)
        otmp = sb("otmp", [P, HALF])
        osum = sb("osum", [P, HALF])
        idn = sb("idn", [P, P])
        gm = sb("gm", [P, P])
        ones = sb("ones", [P, P])
        vec = sb("vec", [P, 14, KT])
        der = sb("der", [P, 4, KT])
        bb = sb("bb", [P, KT])
        t0 = sb("t0", [P, 1])
        bst = sb("bst", [P, KT, NH, 6])
        mv = sb("mv", [P, KT, 2])
        gs = sb("gs", [P, 8, KT])
        expo = sb("expo", [P, KT])
        nmax = sb("nmax", [P, 4])
        rmax = sb("rmax", [P, 4])
        pspare = sb("pspare", [P, 3])
        spare = sb("spare", [P, 8])
        rsum = sb("rsum", [P, 2, GRP])
        rinv = sb("rinv", [P, 2, GRP])
        rb = sb("rb", [P, 2, HALF])

        sps = [ctx.enter_context(nc.psum_tensor(f"sps{i}", [P, N], F32)) for i in range(2)]
        tps = [ctx.enter_context(nc.psum_tensor(f"tps{i}", [P, HALF], F32)) for i in range(2)]
        ops = [ctx.enter_context(nc.psum_tensor(f"ops{i}", [P, HALF], F32)) for i in range(2)]

        BQ0, BK0, BV0, BP0, G0, BE0, BQ1, BK1, BV1, BP1, G1, BE1 = range(12)
        KB1, TWC, BO0, BO1 = range(4)
        ptv = pt[:].rearrange("p (l m n) -> p l m n", l=2, m=MT)
        wbig = [pt[:, i * 2 * KT * C:(i + 1) * 2 * KT * C].rearrange("p (l k n) -> p l k n", l=2, k=KT)
                for i in range(2)]
        pts = [[ptv[:, 0], ptv[:, 1]], [pb_hi[:], pb_lo[:]]]
        vpx = vp[:].rearrange("p m (x d) -> p m x d", x=4)
        v32x = v32[:].rearrange("p m (q e d) -> p m q e d", q=PAIRS, e=2)
        wqkf = wqk[:].rearrange("p l k n -> p (l k n)").bitcast(F32)
        wpf = wp[:].rearrange("p l n -> p (l n)").bitcast(F32)
        wvf = pt[:, 0:2 * KT * C].bitcast(F32)
        LOW, HIGH = slice(0, HD), slice(HD, P)
        own = (LOW, HIGH)
        other = (HIGH, LOW)

        s_ready = [sem("s_ready0"), sem("s_ready1")]
        s_free = [sem("s_free0"), sem("s_free1")]
        t_ready = [sem("t_ready0"), sem("t_ready1")]
        t_done = sem("t_done")
        hi_done = sem("hi_done")
        o_ready = [sem("o_ready0"), sem("o_ready1")]
        o_done = sem("o_done")
        raw_max = sem("raw_max")
        maxed = sem("maxed")
        inv_done = sem("inv_done")
        r_mid = sem("r_mid")
        r_in = sem("r_in")
        o_moved = sem("o_moved")
        rb_free = sem("rb_free")
        o_hi = sem("o_hi")
        o_split = sem("o_split")
        o_scaled = sem("o_scaled")
        ev_hi = sem("ev_hi")
        first_head = sem("first_head")
        k_dup = sem("k_dup")
        vp_done = sem("vp_done")
        gn_step = sem("gn_step")
        gn_stat = sem("gn_stat")
        gn_pow = sem("gn_pow")
        gn_coef = sem("gn_coef")
        gn_val = sem("gn_val")
        gn_hi = sem("gn_hi")
        gn_lo = sem("gn_lo")
        x_in = sem("x_in")
        y_in = sem("y_in")
        wqk_in = sem("wqk_in")
        wp_in = sem("wp_in")
        wv_in = sem("wv_in")
        m_in = sem("m_in")
        y_out = sem("y_out")
        c_in = sem("c_in")
        p_in = sem("p_in")
        p_hi = sem("p_hi")
        p_lo = sem("p_lo")
        p_out = sem("p_out")
        p_mm = sem("p_mm")
        p_vec = sem("p_vec")
        p_one = sem("p_one")

        def s_unit(b, u):
            return u % 2, b * (S_BATCH // 2) + u // 2

        def s_pair(b, p, j):
            return j % 2, b * (S_BATCH // 2) + p * (S_PAIR // 2) + (S_PRE + j) // 2

        def o_unit(b, u):
            return u % 2, b * (O_BATCH // 2) + 1 + u // 2

        def o_count(b, u):
            return b * O_BATCH + 2 + u + 1 + 2

        block = ctx.enter_context(nc.Block())
        stages = [(wq0,), (wk0,), (wv0,), (wp0,), (wk1, wq1), (wv1, wp1)]
        loaded = [16 * sum(len(w) for w in stages[:n + 1]) for n in range(len(stages))]
        stores = [2 * k for k in (PAIRS + 1, PAIRS + 1, 1, PAIRS, 1, 1)]
        stored = [16 * sum(stores[:n + 1]) for n in range(len(stages))]

        @block.sync
        def _(sp):
            for i, a in enumerate((bq0, bk0, bv0, bp0, g0, be0, bq1, bk1, bv1, bp1, g1, be1)):
                sp.dma_start(vec[:, i, :], a).then_inc(c_in, 16)
            sp.dma_start(idn[:], ident).then_inc(c_in, 16)
            sp.dma_start(gm[:], gmean).then_inc(c_in, 16)
            for n, weights in enumerate(stages):
                if n:
                    sp.wait_ge(p_lo, KT * n)
                if n == 4:
                    sp.wait_ge(p_mm, 1)
                for dst, w in zip((xin, y), weights):
                    sp.dma_start(dst[:, :, 0:C], w.rearrange("(k p) n -> p k n", p=P)).then_inc(p_in, 16)
                sp.wait_ge(p_lo, KT * (n + 1))
                for l in range(2):
                    src = xn[:, l, :, 0:C].bitcast(F32)
                    if n < 2:
                        for p in range(PAIRS + 1):
                            dst = WQK_D[p].rearrange("p (l k n) -> p l k n", l=2, k=KT)
                            q = p % PAIRS
                            sp.dma_start(dst[:, l, :, n * P:(n + 1) * P],
                                         src[:, :, q * P:(q + 1) * P]).then_inc(p_out, 16)
                    elif n == 3:
                        for p in range(PAIRS):
                            sp.dma_start(WP_D[p].rearrange("p (l n) -> p l n", l=2)[:, l, :],
                                         src[:, p, :]).then_inc(p_out, 16)
                    else:
                        dst = {2: WV_D, 4: M1_D, 5: M2_D}[n]
                        sp.dma_start(dst.rearrange("p (l k n) -> p l k n", l=2, k=KT)[:, l],
                                     src).then_inc(p_out, 16)
            sp.wait_ge(p_out, stored[-1])
            sp.dma_start(xin[:], x[0]).then_inc(x_in, 16)
            sp.dma_start(wvf, WV_D).then_inc(wv_in, 16)
            sp.dma_start(wqkf, WQK_D[0]).then_inc(wqk_in, 16)
            sp.dma_start(wpf, WP_D[0]).then_inc(wp_in, 16)
            sp.wait_ge(x_in, 16)
            sp.dma_start(y[:], xin[:]).then_inc(y_in, 16)

            def spread_inverse(c, slot):
                sp.wait_ge(rb_free, c + 1)
                sp.wait_ge(inv_done, c + 1)
                sp.dma_start(R_D[slot].rearrange("g p -> p g"), rinv[:, slot, :],
                             allow_slow_non_contiguous=True).then_inc(r_mid, 16)
                sp.wait_ge(r_mid, 16 * (c + 1))
                src = R_D[slot].rearrange("g p -> (g p)").rearrange("(a n) -> a n", a=1)
                sp.dma_start(rb[:, slot, :], src.broadcast_to([P, HALF])).then_inc(r_in, 16)

            def after_qk(k_unit, q_unit, weights):
                sp.wait_ge(s_free[k_unit[0]], k_unit[1] + 2)
                for t in range(2, 6):
                    a, z = own[t % 2], other[t % 2]
                    sp.dma_start(kq[z, t, :].bitcast(F32), kq[a, t, :].bitcast(F32)).then_inc(k_dup, 16)
                sp.wait_ge(s_ready[q_unit[0]], q_unit[1] + 1)
                sp.dma_start(wqkf, weights).then_inc(wqk_in, 16)

            with sp.Fori(0, B) as b:
                following = sp.snap((b + 1) % B)
                after_qk(s_unit(b, 0), s_unit(b, 1), WQK_D[1])
                with sp.Fori(0, PAIRS - 1) as p:
                    for g in range(4):
                        spread_inverse(b * R_BATCH + p * 4 + g, g % 2)
                    after_qk(s_pair(b, p, BLK), s_pair(b, p, BLK + 1), WQK_D[p + 2])
                    proj = s_pair(b, p, BLK + 1 + KT)
                    sp.wait_ge(s_ready[proj[0]], proj[1] + 1)
                    sp.dma_start(wpf, WP_D[p + 1]).then_inc(wp_in, 16)
                for g in range(4):
                    spread_inverse(b * R_BATCH + 4 * (PAIRS - 1) + g, g % 2)
                pv = o_unit(b, O_GN1 - 2)
                sp.wait_ge(o_ready[pv[0]], pv[1] + 1)
                sp.dma_start(pt[:, 0:2 * KT * C].bitcast(F32), M1_D).then_inc(m_in, 16)
                sp.dma_start(pt[:, 2 * KT * C:].bitcast(F32), M2_D).then_inc(m_in, 16)
                pv = o_unit(b, O_GN1 - 1)
                sp.wait_ge(y_in, b * 16 + 16)
                sp.wait_ge(o_ready[pv[0]], pv[1] + 1)
                sp.dma_start(xin[:], x[bass.ds(following, 1)].rearrange("b p k n -> (b p) k n")).then_inc(x_in, 16)
                proj = s_unit(b, S_POST - 1)
                sp.wait_ge(s_ready[proj[0]], proj[1] + 1)
                sp.dma_start(wpf, WP_D[0]).then_inc(wp_in, 16)
                for h in range(NH):
                    spread_inverse(b * R_BATCH + 4 * PAIRS + h, h)
                    for c in range(KT):
                        if h == NH - 1 and c == KT - 1:
                            bank, n = o_unit(b, O_BATCH - 1)
                            sp.wait_ge(o_ready[bank], n + 1)
                            sp.dma_start(wvf, WV_D).then_inc(wv_in, 16)
                        sp.wait_ge(o_done, o_count(b, O_PV1 + h * KT + c))
                        cols = slice(h * HALF, (h + 1) * HALF)
                        sp.dma_start(out[b, :, c, cols], y[:, c, cols]).then_inc(y_out, 16)
                sp.wait_ge(x_in, b * 16 + 32)
                sp.wait_ge(y_out, b * (16 * KT * NH) + 16 * KT * NH)
                sp.dma_start(y[:], xin[:]).then_inc(y_in, 16)
            sp.wait_ge(y_in, 16 * (B + 1))
            sp.wait_ge(wv_in, 16 * (B + 1))
            sp.wait_ge(x_in, 16 * (B + 1))
            sp.wait_ge(wqk_in, 16 * (B * PAIRS + 1))
            sp.wait_ge(wp_in, 16 * (B * PAIRS + 1))

        @block.tensor
        def _(pe):
            mm = nc.tensor.matmul
            def by_vector(dst, w, col):
                for c in range(KT):
                    for k in range(KT):
                        ins = mm(dst[:, c:c + 1], w[:, k, c * P:(c + 1) * P], vec[:, col, k:k + 1],
                                 start=k == 0, stop=k == KT - 1)
                return ins

            def product():
                for c in range(KT):
                    for k in range(KT):
                        ins = mm(sps[c // 2][:, c % 2 * HALF:(c % 2 + 1) * HALF], xin[:, k, c * P:(c + 1) * P],
                                 y[:, k, 0:C], start=k == 0, stop=k == KT - 1)
                    ins.then_inc(p_mm, 1)

            pe.wait_ge(c_in, 16 * 14)
            pe.wait_ge(p_in, loaded[3])
            by_vector(ops[0], xin, BV0).then_inc(p_mm, 1)
            pe.wait_ge(p_in, loaded[4])
            pe.wait_ge(p_vec, 1)
            pe.wait_ge(p_one, 1)
            by_vector(ops[1][:, 0:KT], y, BK1)
            by_vector(ops[1][:, KT:2 * KT], xin, BQ1)
            for k in range(KT):
                last = mm(ops[1][:, 2 * KT:2 * KT + 1], ones[:], bb[:, k:k + 1], start=k == 0, stop=k == KT - 1)
            last.then_inc(p_mm, 1)
            product()
            pe.wait_ge(p_in, loaded[5])
            pe.wait_ge(p_lo, 5 * KT)
            pe.wait_ge(p_vec, 3)
            by_vector(ops[0], y, BV1).then_inc(p_mm, 1)
            product()
            pe.wait_ge(p_lo, 6 * KT)
            pe.wait_ge(p_vec, 7 + 2 * KT)

            def s_take(unit):
                pe.wait_ge(s_free[unit[0]], unit[1] + 1)
                return sps[unit[0]]

            def split_mm(dst, left, right):
                n = len(left)
                for k in range(n):
                    for i, (a, w) in enumerate(((0, 0), (0, 1), (1, 0))):
                        ins = mm(dst, left[k][a], right[k][w], start=k == 0 and i == 0,
                                 stop=k == n - 1 and i == 2)
                return ins

            def cut(t, lo, hi):
                return [[t[:, l, k, lo:hi] for l in range(2)] for k in range(KT)]

            def gn_matmul(b, which, u, i):
                bank, n = o_unit(b, u + i)
                pe.wait_ge(o_done, o_count(b, u + i) - 2)
                pe.wait_ge(gn_stat, b * (2 * (KT + 1)) + which * (KT + 1) + KT + i)
                src = mv[:, :, 0] if i == 0 else gs[:, 1, :]
                mm(ops[bank][:, 0:KT], gm[:], src, start=True, stop=True).then_inc(o_ready[bank], 1)

            def two_halves(unit, left, right, arrival=None):
                dst = s_take(unit)
                for k in range(KT):
                    if arrival is not None:
                        pe.wait_ge(gn_lo, arrival + k + 1)
                    for h in range(2):
                        for i, (a, w) in enumerate(((0, 0), (0, 1), (1, 0))):
                            last = mm(dst[:, h * HALF:(h + 1) * HALF], left(h, k, a), right(h, k, w),
                                      start=k == 0 and i == 0, stop=k == KT - 1 and i == 2)
                last.then_inc(s_ready[unit[0]], 1)

            def v_units(b, first, w, arrival=None):
                for m in range(0, MT, 2):
                    two_halves(s_unit(b, first + m // 2), lambda h, k, a: xn[:, a, k, (m + h) * P:(m + h + 1) * P],
                               lambda h, k, l: w[:, l, k, :], arrival if m == 0 else None)

            def channel_unit(unit, w, lo, arrival=None):
                two_halves(unit, lambda h, k, a: w[:, a, k, lo:lo + P],
                           lambda h, k, l: xn[:, l, k, h * HALF:(h + 1) * HALF], arrival)

            def scores0(unit, i):
                head, m = i // MT, i % MT
                dst = s_take(unit)
                for h in range(NH):
                    for l in range(2):
                        last = mm(dst[:, h * HALF:(h + 1) * HALF], kq[:, head, m * P:(m + 1) * P],
                                  kq[:, 2 + 2 * l + head, h * HALF:(h + 1) * HALF], start=l == 0, stop=l == 1)
                last.then_inc(s_ready[unit[0]], 1)

            def transposes(t, unit, i):
                pe.wait_ge(s_free[unit[0]], unit[1] + 2)
                for h in range(2):
                    pe.wait_ge(t_done, t + h + 1)
                    for j in range(4):
                        last = nc.tensor.transpose(tps[h][:, j * P:(j + 1) * P],
                                                   pr[:, i % 2, (4 * h + j) * P:(4 * h + j + 1) * P], idn[:])
                    last.then_inc(t_ready[h], 1)

            def pv0(b, p, g, tiles):
                if tiles[0] == 0:
                    if g == 0:
                        pe.wait_ge(vp_done, b * PAIRS + p + 1)
                    pe.wait_ge(o_done, b * O_BATCH + p * 4 + (2 + g + 1))
                    pe.wait_ge(t_done, b * T_BATCH + p * T_PAIR + (2 * GRP * (g + 1) + 2))
                head = g // 2
                for m in tiles:
                    for l in range(2):
                        last = mm(ops[g % 2][:], vp[:, m, head * P:(head + 1) * P], pts[g % 2][l][:, m, :],
                                  start=m == 0 and l == 0, stop=m == MT - 1 and l == 1)
                if tiles[-1] == MT - 1:
                    last.then_inc(o_ready[g % 2], 1)

            def projection(b, p, h, units):
                pe.wait_ge(o_split, b * G_BATCH + p * 4 + (h + 3 + 1))
                for j, unit in enumerate(units):
                    dst = s_take(unit)
                    for c in range(2):
                        t = 2 * j + c
                        last = split_mm(dst[:, c * HALF:(c + 1) * HALF],
                                        [[wp[:, l, t * P:(t + 1) * P] for l in range(2)]],
                                        [[kq[:, 6 + l, h * HALF:(h + 1) * HALF] for l in range(2)]])
                    last.then_inc(s_ready[unit[0]], 1)

            def pair(b, p, unit_of, more):
                pe.wait_ge(k_dup, b * (64 * PAIRS) + p * 64 + 64)
                scores0(unit_of(0), 0)
                scores0(unit_of(1), 1)
                for i in range(BLK):
                    if i + 2 < BLK:
                        scores0(unit_of(i + 2), i + 2)
                    transposes(b * T_BATCH + p * T_PAIR + 2 * i, unit_of(i), i)
                    if i >= GRP:
                        share = MT // GRP
                        pv0(b, p, i // GRP - 1, range(i % GRP * share, (i % GRP + 1) * share))
                at = BLK
                if more:
                    pe.wait_ge(wqk_in, b * (16 * PAIRS) + p * 16 + 32)
                    channel_unit(unit_of(BLK), wqk, P)
                pv0(b, p, 3, range(MT))
                if more:
                    channel_unit(unit_of(BLK + 1), wqk, 0)
                    at += 2
                pe.wait_ge(wp_in, b * (16 * PAIRS) + p * 16 + 16)
                projection(b, p, 0, (unit_of(at), unit_of(at + 1)))
                projection(b, p, 1, (unit_of(at + 2), unit_of(at + 3)))

            gn_matmul(0, 0, -2, 0)
            gn_matmul(0, 0, -2, 1)
            with pe.Fori(0, B) as b:
                pe.wait_ge(wqk_in, b * (16 * PAIRS) + 16)
                channel_unit(s_unit(b, 0), wqk, P, b * (2 * KT))
                channel_unit(s_unit(b, 1), wqk, 0)
                pe.wait_ge(wv_in, b * 16 + 16)
                v_units(b, 2, wbig[0])
                with pe.Fori(0, PAIRS - 1) as p:
                    pair(b, p, lambda j: s_pair(b, p, j), True)
                pair(b, PAIRS - 1, lambda j: s_unit(b, S_PRE + (PAIRS - 1) * S_PAIR + j), False)

                gn_matmul(b, 1, O_GN1, 0)
                gn_matmul(b, 1, O_GN1, 1)
                pe.wait_ge(m_in, b * 32 + 32)
                for c in range(KT):
                    channel_unit(s_unit(b, S_POST + c), wbig[0], c * P, b * (2 * KT) + KT if c == 0 else None)
                for h in range(NH):
                    pe.wait_ge(t_done, b * T_BATCH + (T_POST + h + 1))
                    split_mm(tps[h][:], cut(tw, 0, P), cut(xn, h * HALF, (h + 1) * HALF)).then_inc(t_ready[h], 1)
                v_units(b, S_POST + KT, wbig[1])

                def scores1(i):
                    unit = s_unit(b, S_POST + KT + MT // 2 + i)
                    dst = s_take(unit)
                    for h in range(NH):
                        last = split_mm(dst[:, h * HALF:(h + 1) * HALF], cut(xn, i * P, (i + 1) * P),
                                        [[kq[:, l * KT + k, h * HALF:(h + 1) * HALF] for l in range(2)]
                                         for k in range(KT)])
                    last.then_inc(s_ready[unit[0]], 1)

                def pv1(h):
                    pe.wait_ge(t_done, b * T_BATCH + (T_POST + 2 + 2 * GRP * (h + 1) + 2))
                    for c in range(KT):
                        bank, n = o_unit(b, O_PV1 + h * KT + c)
                        pe.wait_ge(o_done, o_count(b, O_PV1 + h * KT + c) - 2)
                        split_mm(ops[bank][:],
                                 [[v[:, m, l * C + c * P:l * C + (c + 1) * P] for l in range(2)] for m in range(MT)],
                                 [[ptv[:, l, m, :] for l in range(2)] for m in range(MT)]).then_inc(o_ready[bank], 1)

                scores1(0)
                scores1(1)
                for i in range(MT):
                    if i + 2 < MT:
                        scores1(i + 2)
                    if i == GRP:
                        gn_matmul(b, 2, O_GN0, 1)
                        pv1(0)
                    transposes(b * T_BATCH + (T_POST + 2 + 2 * i), s_unit(b, S_POST + KT + MT // 2 + i), i)
                    if i == GRP - 1:
                        gn_matmul(b, 2, O_GN0, 0)
                pv1(1)

        @block.scalar
        def _(act):
            def hi_of(dst, src, bias, sem, scale=1.0):
                nc.scalar.activation(dst, src, ACT.Identity, bias=bias, scale=scale).then_inc(sem, 1)

            def group_norm(b, src, which):
                act.wait_ge(gn_coef, b * 2 + (which + 1))
                for k in range(KT):
                    hi_of(xn[:, 0, k, :], src[:, k, :], gs[:, 3, k:k + 1], gn_hi, gs[:, 6, k:k + 1])

            def filled(unit):
                act.wait_ge(s_ready[unit[0]], unit[1] + 1)
                return sps[unit[0]]

            def exp(i, m, unit, free):
                act.wait_ge(maxed, m + 1)
                if free is not None:
                    act.wait_ge(t_ready[1], free)
                nc.scalar.activation(pr[:, i % 2, :], sps[unit[0]][:], ACT.Exp, bias=nmax[:, i % 4:i % 4 + 1],
                                     accum_out=rsum[:, i // GRP % 2, i % GRP:i % GRP + 1]).then_inc(s_free[unit[0]], 1)

            def p_hi(t, i, buf):
                for h in range(2):
                    act.wait_ge(t_ready[h], t + 1)
                    dst = pts[buf][0][:, 4 * h:4 * h + 4, i % GRP * P:(i % GRP + 1) * P]
                    nc.scalar.activation(dst, tps[h][:].rearrange("p (m n) -> p m n", m=4),
                                         ACT.Identity, bias=0.0).then_inc(hi_done, 1)

            def move(b, p, g):
                e = g // 2
                act.wait_ge(o_ready[g % 2], b * (O_BATCH // 2) + p * 2 + (1 + g // 2 + 1))
                act.wait_ge(o_done, b * O_BATCH + p * 4 + (2 + g + 2))
                nc.scalar.activation(otmp[own[e], :], ops[g % 2][other[e], :], ACT.Identity,
                                     bias=0.0).then_inc(o_moved, 1)

            def v_hi(p):
                src = v32x[:, :, p] if isinstance(p, int) else v32[:, :, bass.ds(p * 2 * HD, 2 * HD)].rearrange(
                    "p m (e d) -> p m e d", e=2)
                nc.scalar.activation(vpx[:, :, 0::3, :], src, ACT.Identity, bias=0.0).then_inc(ev_hi, 1)

            def qk_hi(unit, slot, col, p):
                src = filled(unit)
                for e in range(2):
                    bias = vec[own[e], col, p:p + 1] if isinstance(p, int) else vec[own[e], col, bass.ds(p, 1)]
                    hi_of(kq[own[e], slot + e, :], src[own[e], :], bias, ev_hi)

            def pair(b, p, unit_of, more):
                tn = b * (T_BATCH // 2) + p * BLK
                m = b * M_BATCH + p * BLK
                exp(0, m, unit_of(0), None)
                exp(1, m + 1, unit_of(1), None)
                for i in range(BLK):
                    g = i // GRP
                    if i % GRP == 0:
                        act.wait_ge(o_ready[g % 2], b * (O_BATCH // 2) + p * 2 + (1 + g // 2))
                    if i == GRP:
                        act.wait_ge(y_in, b * 16 + 16)
                    p_hi(tn + i, i, g % 2)
                    if i + 2 < BLK:
                        exp(i + 2, m + i + 2, unit_of(i + 2), tn + i + 1)
                    if i >= 2 * GRP and i % GRP == 0:
                        move(b, p, g - 2)
                move(b, p, 2)
                if more:
                    qk_hi(unit_of(BLK), 2, BK0, p + 1)
                move(b, p, 3)
                if more:
                    v_hi(p + 1)
                    qk_hi(unit_of(BLK + 1), 0, BQ0, p + 1)

            act.wait_ge(x_in, 16)
            group_norm(0, xin, 0)
            with act.Fori(0, B) as b:
                qk_hi(s_unit(b, 0), 2, BK0, 0)
                qk_hi(s_unit(b, 1), 0, BQ0, 0)
                for u in range(MT // 2):
                    unit = s_unit(b, 2 + u)
                    src = filled(unit)
                    nc.scalar.activation(v32[:, 2 * u:2 * u + 2, :], src[:].rearrange("p (m c) -> p m c", m=2),
                                         ACT.Identity, bias=0.0).then_inc(s_free[unit[0]], 1)
                for u in range(S_PRE - 2, S_PRE):
                    unit = s_unit(b, u)
                    act.wait_ge(s_free[unit[0]], unit[1] + 2)
                v_hi(0)
                with act.Fori(0, PAIRS - 1) as p:
                    pair(b, p, lambda j: s_pair(b, p, j), True)
                pair(b, PAIRS - 1, lambda j: s_unit(b, S_PRE + (PAIRS - 1) * S_PAIR + j), False)

                group_norm(b, y, 1)
                for c in range(KT):
                    hi_of(kq[:, c, :], filled(s_unit(b, S_POST + c))[:], der[:, KB1, c:c + 1], ev_hi)
                for u in range(MT // 2):
                    src = filled(s_unit(b, S_POST + KT + u))
                    nc.scalar.activation(v[:, 2 * u:2 * u + 2, 0:C], src[:].rearrange("p (m c) -> p m c", m=2),
                                         ACT.Identity, bias=0.0).then_inc(ev_hi, 1)
                first = S_POST + KT + MT // 2
                tn = b * (T_BATCH // 2) + (T_POST // 2 + 1)
                m = b * M_BATCH + PAIRS * BLK
                exp(0, m, s_unit(b, first), None)
                exp(1, m + 1, s_unit(b, first + 1), None)
                for i in range(MT):
                    if i == GRP:
                        bank, n = o_unit(b, O_PV1 + KT - 1)
                        act.wait_ge(o_ready[bank], n + 1)
                    p_hi(tn + i, i, 0)
                    if i + 2 < MT:
                        exp(i + 2, m + i + 2, s_unit(b, first + i + 2), tn + i + 1)
                group_norm(b, xin, 2)

        @block.vector
        def _(dve):
            op = nc.vector
            op.memset(ones[:], 1.0).then_inc(p_one, 1)
            op.memset(expo[:], -0.5).then_inc(p_one, 1)
            for n, s in enumerate((s_free[0], s_free[1], t_done, t_done, o_done, o_done)):
                op.memset(spare[:, n:n + 1], 0.0).then_inc(s, 1)
            dve.wait_ge(c_in, 16 * 14)
            dve.wait_ge(p_one, 2)
            op.tensor_tensor(bb[:], vec[:, BQ1, :], vec[:, BK1, :], ALU.mult).then_inc(p_vec, 1)
            op.tensor_scalar(vec[:, BQ0, :], vec[:, BQ0, :], SCALE0, None, ALU.mult).then_inc(p_vec, 1)

            for n in range(len(stages)):
                dve.wait_ge(p_in, loaded[n])
                if n:
                    dve.wait_ge(p_out, stored[n - 1])
                scale = {0: SCALE0, 4: SCALE1}.get(n, 1.0)
                if n == 4:
                    dve.wait_ge(p_mm, 1)
                    op.tensor_tensor(der[:, BO0, :], ops[0][:, 0:KT], vec[:, BP0, :], ALU.add).then_inc(p_vec, 1)
                    dve.wait_ge(p_mm, 2)
                    op.tensor_scalar(der[:, KB1, :], ops[1][:, 0:KT], SCALE1, None, ALU.mult).then_inc(p_vec, 1)
                    op.tensor_scalar(der[:, TWC, :], ops[1][:, KT:2 * KT], SCALE1, None, ALU.mult).then_inc(p_vec, 1)
                    op.tensor_scalar(t0[:], ops[1][:, 2 * KT:2 * KT + 1], SCALE1, None, ALU.mult).then_inc(p_vec, 1)
                    dve.wait_ge(p_vec, 6)
                    for k in range(KT):
                        op.tensor_scalar(tw[:, 0, k, :], ones[:], der[:, TWC, k:k + 1], None, ALU.mult).then_inc(p_vec, 1)
                    dve.wait_ge(p_vec, 6 + KT)
                    for k in range(KT):
                        op.scalar_tensor_tensor(out=tw[:, 1, k, :], in0=ones[:], scalar=der[:, TWC, k:k + 1],
                                                in1=tw[:, 0, k, :].bitcast(F32), op0=ALU.mult,
                                                op1=ALU.subtract).then_inc(p_vec, 1)
                if n == 5:
                    dve.wait_ge(p_mm, 2 + KT + 1)
                    op.tensor_tensor(der[:, BO1, :], ops[0][:, 0:KT], vec[:, BP1, :], ALU.add).then_inc(p_vec, 1)
                for k in range(KT):
                    if n < 4:
                        src = xin[:, k, 0:C]
                    else:
                        dve.wait_ge(p_mm, (2 if n == 4 else 3 + KT) + k + 1)
                        src = sps[k // 2][:, k % 2 * HALF:(k % 2 + 1) * HALF]
                    op.tensor_scalar(xn[:, 0, k, 0:C], src, scale, None, ALU.mult).then_inc(p_hi, 1)
                    dve.wait_ge(p_hi, KT * n + k + 1)
                    op.scalar_tensor_tensor(out=xn[:, 1, k, 0:C], in0=src, scalar=scale,
                                            in1=xn[:, 0, k, 0:C].bitcast(F32), op0=ALU.mult,
                                            op1=ALU.subtract).then_inc(p_lo, 1)
            dve.wait_ge(p_vec, 7 + 2 * KT)
            dve.wait_ge(p_out, stored[-1])

            def filled(unit):
                dve.wait_ge(s_ready[unit[0]], unit[1] + 1)
                return sps[unit[0]]

            def gn_stats(src, k, h):
                op.bn_stats(bst[:, k, h, :], src[:, k, h * HALF:(h + 1) * HALF]).then_inc(gn_step, 1)

            def gn_mean(b, which):
                dve.wait_ge(gn_step, b * (2 * GN_STEPS) + (which * GN_STEPS + NH * KT))
                op.memset(spare[:, 6:7], 0.0)
                for k in range(KT):
                    op.bn_aggr(mv[:, k, :], bst[:, k, :, :].rearrange("p h s -> p (h s)")).then_inc(gn_stat, 1)

            def gn_deviation(b, which, u):
                step0 = b * (2 * GN_STEPS) + (which * GN_STEPS + NH * KT)
                dve.wait_ge(gn_stat, b * (2 * (KT + 1)) + (which * (KT + 1) + KT))
                bank, n = o_unit(b, u)
                dve.wait_ge(o_ready[bank], n + 1)
                op.tensor_tensor(gs[:, 0, :], mv[:, :, 0], ops[bank][:, 0:KT], ALU.subtract).then_inc(gn_step, 1)
                op.tensor_copy(gs[:, 2, :], ops[bank][:, 0:KT]).then_inc(o_done, 1)
                dve.wait_ge(gn_step, step0 + 1)
                op.tensor_tensor(gs[:, 4, :], gs[:, 0, :], gs[:, 0, :], ALU.mult).then_inc(gn_step, 1)
                dve.wait_ge(gn_step, step0 + 2)
                op.tensor_tensor(gs[:, 1, :], gs[:, 4, :], mv[:, :, 1], ALU.add).then_inc(gn_stat, 1)

            def gn_variance(b, u, eps):
                bank, n = o_unit(b, u + 1)
                dve.wait_ge(o_ready[bank], n + 1)
                op.tensor_scalar(gs[:, 5, :], ops[bank][:, 0:KT], eps, None, ALU.add).then_inc(o_done, 1)

            def gn_coefficients(b, which, u, gamma, beta):
                step0 = b * (2 * GN_STEPS) + (which * GN_STEPS + NH * KT)
                dve.wait_ge(gn_pow, b * 2 + (which + 1))
                op.tensor_tensor(gs[:, 6, :], gs[:, 7, :], vec[:, gamma, :], ALU.mult).then_inc(gn_step, 1)
                dve.wait_ge(o_done, o_count(b, u))
                dve.wait_ge(gn_step, step0 + 3)
                op.tensor_tensor(gs[:, 4, :], gs[:, 2, :], gs[:, 6, :], ALU.mult).then_inc(gn_step, 1)
                dve.wait_ge(gn_step, step0 + 4)
                op.tensor_tensor(gs[:, 3, :], vec[:, beta, :], gs[:, 4, :], ALU.subtract).then_inc(gn_coef, 1)
                dve.wait_ge(gn_coef, b * 2 + (which + 1))

            def gn_apply(b, which, src, k):
                done = b * (2 * KT) + (which * KT + k)
                if k >= 2:
                    dve.wait_ge(gn_lo, done - 1)
                op.tensor_scalar(pr[:, k % 2, :], src[:, k, :], gs[:, 6, k:k + 1], gs[:, 3, k:k + 1],
                                 ALU.mult, ALU.add).then_inc(gn_val, 1)
                dve.wait_ge(gn_val, done + 1)
                dve.wait_ge(gn_hi, done + 1)
                op.tensor_tensor(xn[:, 1, k, :], pr[:, k % 2, :], xn[:, 0, k, :].bitcast(F32),
                                 ALU.subtract).then_inc(gn_lo, 1)

            def lo_of(dst, src, bias, hi, sem):
                op.scalar_tensor_tensor(out=dst, in0=src, scalar=bias, in1=hi.bitcast(F32), op0=ALU.add,
                                        op1=ALU.subtract).then_inc(sem, 1)

            def vec_of(col, e, p):
                return vec[own[e], col, p:p + 1] if isinstance(p, int) else vec[own[e], col, bass.ds(p, 1)]

            def k_lo(unit, e0, p):
                src = filled(unit)
                for e in range(2):
                    dve.wait_ge(ev_hi, e0 + e + 1)
                    lo_of(kq[own[e], 4 + e, :], src[own[e], :], vec_of(BK0, e, p), kq[own[e], 2 + e, :],
                          s_free[unit[0]] if e else first_head)

            def q_lo(unit, e0, p):
                src = filled(unit)
                for e in range(2):
                    dve.wait_ge(ev_hi, e0 + e + 1)
                    lo_of(kq[other[e], e, :], src[own[e], :], vec_of(BQ0, e, p), kq[own[e], e, :],
                          s_free[unit[0]] if e else first_head)

            def v_lo(e0, p):
                src = v32x[:, :, p] if isinstance(p, int) else v32[:, :, bass.ds(p * 2 * HD, 2 * HD)].rearrange(
                    "p m (e d) -> p m e d", e=2)
                dve.wait_ge(ev_hi, e0 + 1)
                op.tensor_tensor(vpx[:, :, 1:3, :], src, vpx[:, :, 0::3, :].bitcast(F32),
                                 ALU.subtract).then_inc(vp_done, 1)

            def row_max(unit, m, i):
                src = filled(unit)
                op.tensor_reduce(out=nmax[:, i % 4:i % 4 + 1], in_=src[:], axis=AX.X, op=ALU.max,
                                 negate=True).then_inc(maxed, 1)

            def p_lo_part(m, i, buf):
                for h in range(2):
                    dve.wait_ge(hi_done, m * 2 + h + 1)
                    cols = slice(i % GRP * P, (i % GRP + 1) * P)
                    hi, lo = (t[:, 4 * h:4 * h + 4, cols] for t in pts[buf])
                    op.tensor_tensor(lo, tps[h][:].rearrange("p (m n) -> p m n", m=4), hi.bitcast(F32),
                                     ALU.subtract).then_inc(t_done, 1)

            def inverse(unit, i, sent=None):
                if sent is not None:
                    dve.wait_ge(r_mid, sent)
                dve.wait_ge(s_free[unit[0]], unit[1] + 2)
                slot = i // GRP % 2
                op.reciprocal(rinv[:, slot, :], rsum[:, slot, :]).then_inc(inv_done, 1)

            def joined(b, p, g):
                e = g // 2
                c = b * G_BATCH + p * 4 + g
                dve.wait_ge(o_moved, c + 1)
                dve.wait_ge(o_split, c + 1)
                op.tensor_tensor(osum[own[e], :], ops[g % 2][own[e], :], otmp[own[e], :], ALU.add).then_inc(o_done, 1)

            def add_projection(b, h, units, last):
                cols = slice(h * HALF, (h + 1) * HALF)
                for j, unit in enumerate(units):
                    src = filled(unit)
                    if not last:
                        two = y[:, 2 * j:2 * j + 2, cols]
                        op.tensor_tensor(two, src[:].rearrange("p (c n) -> p c n", c=2), two,
                                         ALU.add).then_inc(s_free[unit[0]], 1)
                        continue
                    for c in range(2):
                        t = 2 * j + c
                        op.scalar_tensor_tensor(out=y[:, t, cols], in0=src[:, c * HALF:(c + 1) * HALF],
                                                scalar=der[:, BO0, t:t + 1], in1=y[:, t, cols], op0=ALU.add,
                                                op1=ALU.add).then_inc(s_free[unit[0]] if c else first_head, 1)
                    dve.wait_ge(s_free[unit[0]], unit[1] + 2)
                    for c in range(2):
                        gn_stats(y, 2 * j + c, h)

            def pair(b, p, unit_of, more):
                m = b * M_BATCH + p * BLK
                row_max(unit_of(0), m, 0)
                row_max(unit_of(1), m + 1, 1)
                for i in range(BLK):
                    if i + 2 < BLK:
                        row_max(unit_of(i + 2), m + i + 2, i + 2)
                    if i > 2 * GRP and i % GRP == 1:
                        joined(b, p, i // GRP - 2)
                    if i % GRP == GRP - 1:
                        g = i // GRP
                        inverse(unit_of(i), i, b * (16 * R_BATCH) + p * 64 + 16 * (g - 1) if g >= 2 else None)
                    p_lo_part(m + i, i, i // GRP % 2)
                dve.wait_ge(y_in, b * 16 + 16)
                e0 = b * E_BATCH + p * E_PAIR + E_PAIR
                joined(b, p, 2)
                if more:
                    k_lo(unit_of(BLK), e0, p + 1)
                joined(b, p, 3)
                at = BLK
                if more:
                    v_lo(e0 + 2, p + 1)
                    q_lo(unit_of(BLK + 1), e0 + 3, p + 1)
                    at += 2
                add_projection(b, 0, (unit_of(at), unit_of(at + 1)), not more)
                add_projection(b, 1, (unit_of(at + 2), unit_of(at + 3)), not more)

            dve.wait_ge(x_in, 16)
            for k in range(KT):
                for h in range(NH):
                    gn_stats(xin, k, h)
            gn_mean(0, 0)
            gn_deviation(0, 0, -2)
            gn_variance(0, -2, EPS0)
            gn_coefficients(0, 0, -2, G0, BE0)
            for k in range(KT):
                gn_apply(0, 0, xin, k)
            with dve.Fori(0, B) as b:
                k_lo(s_unit(b, 0), b * E_BATCH, 0)
                q_lo(s_unit(b, 1), b * E_BATCH + 2, 0)
                v_lo(b * E_BATCH + 4, 0)
                with dve.Fori(0, PAIRS - 1) as p:
                    pair(b, p, lambda j: s_pair(b, p, j), True)
                pair(b, PAIRS - 1, lambda j: s_unit(b, S_PRE + (PAIRS - 1) * S_PAIR + j), False)

                gn_mean(b, 1)
                gn_deviation(b, 1, O_GN1)
                gn_variance(b, O_GN1, EPS1)
                gn_coefficients(b, 1, O_GN1, G1, BE1)
                for k in range(KT):
                    gn_apply(b, 1, y, k)
                for c in range(KT):
                    unit = s_unit(b, S_POST + c)
                    src = filled(unit)
                    dve.wait_ge(ev_hi, b * E_BATCH + (E_K1 + c + 1))
                    lo_of(kq[:, KT + c, :], src[:], der[:, KB1, c:c + 1], kq[:, c, :], s_free[unit[0]])
                for h in range(NH):
                    dve.wait_ge(t_ready[h], b * (T_BATCH // 2) + (T_POST // 2 + 1))
                    op.tensor_scalar(trow[:, h * HALF:(h + 1) * HALF], tps[h][:], t0[:], None, ALU.add).then_inc(t_done, 1)
                for u in range(MT // 2):
                    unit = s_unit(b, S_POST + KT + u)
                    src = filled(unit)
                    dve.wait_ge(ev_hi, b * E_BATCH + (E_V1 + u + 1))
                    op.tensor_tensor(v[:, 2 * u:2 * u + 2, C:], src[:].rearrange("p (m c) -> p m c", m=2),
                                     v[:, 2 * u:2 * u + 2, 0:C].bitcast(F32), ALU.subtract).then_inc(s_free[unit[0]], 1)
                dve.wait_ge(t_done, b * T_BATCH + (T_POST + 2 + 2))
                m = b * M_BATCH + PAIRS * BLK

                def row_max1(i):
                    unit = s_unit(b, S_POST + KT + MT // 2 + i)
                    src = filled(unit)
                    op.memset(spare[:, 7:8], 0.0)
                    op.tensor_tensor_reduce(out=src[:], in0=src[:], in1=trow[:], scale=1.0, scalar=LOWEST,
                                            op0=ALU.add, op1=ALU.max,
                                            accum_out=rmax[:, i % 4:i % 4 + 1]).then_inc(raw_max, 1)
                    dve.wait_ge(raw_max, b * MT + i + 1)
                    op.tensor_scalar(nmax[:, i % 4:i % 4 + 1], rmax[:, i % 4:i % 4 + 1], -1.0, None,
                                     ALU.mult).then_inc(maxed, 1)

                def residual(h, c):
                    if c == 0:
                        dve.wait_ge(r_in, b * (16 * R_BATCH) + 16 * (4 * PAIRS + h + 1))
                    u = O_PV1 + h * KT + c
                    bank, n = o_unit(b, u)
                    cols = slice(h * HALF, (h + 1) * HALF)
                    dve.wait_ge(o_ready[bank], n + 1)
                    op.tensor_tensor(osum[:], ops[bank][:], rb[:, h, :], ALU.mult).then_inc(o_scaled, 1)
                    dve.wait_ge(o_scaled, b * (NH * KT) + (h * KT + c + 1))
                    op.scalar_tensor_tensor(out=y[:, c, cols], in0=osum[:], scalar=der[:, BO1, c:c + 1],
                                            in1=y[:, c, cols], op0=ALU.add, op1=ALU.add).then_inc(o_done, 1)
                    dve.wait_ge(o_done, o_count(b, u))
                    if c == KT - 1:
                        op.memset(spare[:, 0:1], 0.0).then_inc(rb_free, 1)

                row_max1(0)
                row_max1(1)
                for i in range(MT):
                    if i + 2 < MT:
                        row_max1(i + 2)
                    if i == 1:
                        dve.wait_ge(x_in, b * 16 + 32)
                    if i in (1, 2):
                        for k in (2 * i - 2, 2 * i - 1):
                            for h in range(NH):
                                gn_stats(xin, k, h)
                    if i == GRP - 1:
                        gn_mean(b, 2)
                    if i == GRP:
                        gn_variance(b, O_GN0, EPS0)
                        for c in range(KT):
                            residual(0, c)
                    if i == GRP + 1:
                        gn_coefficients(b, 2, O_GN0, G0, BE0)
                    if i % GRP == GRP - 1:
                        inverse(s_unit(b, S_POST + KT + MT // 2 + i), i)
                    p_lo_part(m + i, i, 0)
                    if i == GRP - 1:
                        gn_deviation(b, 2, O_GN0)
                gn_apply(b, 2, xin, 0)
                gn_apply(b, 2, xin, 1)
                residual(1, 0)
                gn_apply(b, 2, xin, 2)
                residual(1, 1)
                gn_apply(b, 2, xin, 3)
                residual(1, 2)
                residual(1, 3)

        @block.gpsimd
        def _(pool):
            op = nc.gpsimd

            def group_norm(b, u):
                pool.wait_ge(o_done, o_count(b, u + 1))
                op.tensor_tensor(gs[:, 7, :], gs[:, 5, :], expo[:], ALU.pow).then_inc(gn_pow, 1)

            def pair(b, p):
                for g in range(4):
                    c = b * G_BATCH + p * 4 + g
                    w = own[g // 2]
                    cols = slice(g % 2 * HALF, (g % 2 + 1) * HALF)
                    pool.wait_ge(o_done, b * O_BATCH + p * 4 + (2 + g + 3))
                    pool.wait_ge(r_in, b * (16 * R_BATCH) + p * 64 + 16 * (g + 1))
                    op.tensor_tensor(kq[w, 6, cols], osum[w, :], rb[w, g % 2, :], ALU.mult).then_inc(o_hi, 1)
                    pool.wait_ge(o_hi, c + 1)
                    op.tensor_tensor(osum[w, :], osum[w, :], rb[w, g % 2, :], ALU.mult).then_inc(rb_free, 1)
                    pool.wait_ge(rb_free, b * R_BATCH + p * 4 + (g + 3))
                    op.tensor_tensor(kq[w, 7, cols], osum[w, :], kq[w, 6, cols].bitcast(F32),
                                     ALU.subtract).then_inc(o_split, 1)

            pool.wait_ge(p_one, 2)
            for n, s in enumerate((o_split, rb_free, rb_free)):
                op.memset(pspare[:, n:n + 1], 0.0).then_inc(s, 1)
            group_norm(0, -2)
            with pool.Fori(0, B) as b:
                with pool.Fori(0, PAIRS) as p:
                    pair(b, p)
                group_norm(b, O_GN1)
                group_norm(b, O_GN0)

    return nc


def kernel(**inputs):
    import numpy as _np
    import concourse.bacc as _bacc
    from concourse import mybir as _mybir
    from concourse.bass_utils import run_bass_kernel_spmd as _run

    def arr(name):
        return _np.asarray(inputs[name])

    def column(a):
        return _np.ascontiguousarray(a.reshape(-1, P).T)

    wqkv, bqkv = arr("L0_conv_w_qkv"), arr("L0_conv_b_qkv")
    xl = arr("x").reshape(B, KT, P, N).transpose(0, 2, 1, 3)
    gmean = _np.kron(_np.eye(P * GROUPS // C), _np.full((C // GROUPS,) * 2, GROUPS / C)).astype(_np.float32)
    given = dict(
        x=xl, wq0=wqkv[0:C].T, wk0=wqkv[C:2 * C].T, wv0=wqkv[2 * C:].T, wp0=arr("L0_conv_w_proj").T,
        bq0=column(bqkv[0:C]), bk0=column(bqkv[C:2 * C]), bv0=column(bqkv[2 * C:]),
        bp0=column(arr("L0_conv_b_proj")), g0=column(arr("L0_conv_gamma")), be0=column(arr("L0_conv_beta")),
        wq1=arr("L1_conv_q_w"), wk1=arr("L1_conv_k_w"), wv1=arr("L1_conv_v_w"), wp1=arr("L1_conv_proj_w").T,
        bq1=column(arr("L1_conv_q_b")), bk1=column(arr("L1_conv_k_b")), bv1=column(arr("L1_conv_v_b")),
        bp1=column(arr("L1_conv_proj_b")), g1=column(arr("L1_conv_gn_gamma")), be1=column(arr("L1_conv_gn_beta")),
        ident=_np.eye(P, dtype=_np.float32), gmean=gmean)
    nc = _bacc.Bacc("TRN2", target_bir_lowering=False, num_devices=1)
    arrays, args = {}, {}
    for name, a in given.items():
        a = _np.ascontiguousarray(a)
        arrays[f"in_{name}"] = a
        args[name] = nc.dram_tensor(f"in_{name}", a.shape, _mybir.dt.from_np(a.dtype), kind="ExternalInput").ap()
    args["out"] = nc.dram_tensor("out_x", (B, P, KT, N), _mybir.dt.float32, kind="ExternalOutput").ap()
    attention_blocks(nc, **args)
    r = _run(nc, [arrays], core_ids=[0])
    got = r.results[0]["out_x"]
    return _np.ascontiguousarray(got.transpose(0, 2, 1, 3)).reshape(B, C, 32, 32)
```

```python
from contextlib import ExitStack

import concourse.bass as bass
from concourse import mybir

ALU = mybir.AluOpType
ACT = mybir.ActivationFunctionType
AX = mybir.AxisListType
F32 = mybir.dt.float32
F32R = mybir.dt.float32r

P = 128
B, C, N = 8, 512, 1024
HEADS, GROUPS = 8, 32
HD = C // HEADS
KT = C // P
MT = N // P
HALF = 512
NH = N // HALF
PAIRS = HEADS // 2
BLK = 2 * MT
GRP = HALF // P
SCALE0 = float(HD) ** -0.5
SCALE1 = float(C) ** -0.5
EPS0, EPS1 = 1e-5, 1e-6
LOWEST = -3.4028234e38

S_PRE = 2 + MT // 2
S_PAIR = BLK + 2
S_POST = S_PRE + (PAIRS - 1) * S_PAIR + BLK
S_BATCH = S_POST + KT + MT // 2 + MT
T_PAIR = 2 * BLK
T_POST = PAIRS * T_PAIR
T_BATCH = T_POST + 2 + 2 * MT
O_PAIR = 4 + NH * KT
O_GN1 = O_PAIR * PAIRS
O_GN0 = O_GN1 + 2
O_PV1 = O_GN0 + 2
O_BATCH = O_PV1 + NH * KT
M_BATCH = PAIRS * BLK + MT
R_BATCH = 4 * PAIRS + NH
G_BATCH = 4 * PAIRS
E_PRE, E_PAIR = 4, 6
E_K1 = E_PRE + (PAIRS - 1) * E_PAIR + 2
E_V1 = E_K1 + KT
E_BATCH = E_V1 + MT // 2
GN_STEPS = NH * KT + 4
assert S_BATCH % 2 == 0 and S_PAIR % 2 == 0 and S_POST % 2 == 0 and T_BATCH % 2 == 0 and O_BATCH % 2 == 0


def attention_blocks(nc, x, wq0, wk0, wv0, wp0, wq1, wk1, wv1, wp1, vectors, ident, gmean, out):
    with ExitStack() as ctx:
        def sb(name, shape, dt=F32):
            return ctx.enter_context(nc.sbuf_tensor(name, shape, dt))

        def sem(name):
            return ctx.enter_context(nc.semaphore(name))

        def dram(name, shape):
            return nc.dram_tensor(name, shape, F32, kind="Internal").ap()

        WQK_D = dram("wqk_split", [PAIRS + 1, P, 2 * KT * 2 * P])
        WV_D = dram("wv_split", [P, 2 * KT * C])
        WP_D = dram("wp_split", [PAIRS, P, 2 * C])
        M1_D = dram("m1_split", [P, 2 * KT * C])
        M2_D = dram("m2_split", [P, 2 * KT * C])
        R_D = dram("inverse_sums", [2, GRP, P])

        base = (nc.sbuf_base + 31) // 32 * 32
        sb("arena", [P, 5 * KT * N])

        def at(name, shape, k, dt=F32):
            return nc.alloc_sbuf_tensor_at(name, shape, dt, offset=base + 4 * k)

        xin = at("xin", [P, KT, N], 0)
        pb_hi = at("pb_hi", [P, MT, HALF], 0, F32R)
        v = at("v", [P, MT, 2 * C], KT * N, F32R)
        v32 = at("v32", [P, MT, C], KT * N)
        pb_lo = at("pb_lo", [P, MT, HALF], 2 * KT * N, F32R)
        xn = at("xn", [P, 2, KT, N], 3 * KT * N, F32R)
        w_raw = at("w_raw", [P, 4, KT, C], 3 * KT * N)
        y = sb("y", [P, KT, N])
        kq = sb("kq", [P, 8, N], F32R)
        pt = sb("pt", [P, 2 * MT * HALF], F32R)
        pr = sb("pr", [P, 2, N])
        vp = sb("vp", [P, MT, 4 * HD], F32R)
        wqk = sb("wqk", [P, 2, KT, 2 * P], F32R)
        wp = sb("wp", [P, 2, C], F32R)
        trow = sb("trow", [P, N])
        tw = sb("tw", [P, 2, KT, P], F32R)
        otmp = sb("otmp", [P, HALF])
        osum = sb("osum", [P, HALF])
        idn = sb("idn", [P, P])
        gm = sb("gm", [P, P])
        ones = sb("ones", [P, P])
        vec = sb("vec", [P, 12, KT])
        der = sb("der", [P, 4, KT])
        bb = sb("bb", [P, KT])
        t0 = sb("t0", [P, 1])
        bst = sb("bst", [P, KT, NH, 6])
        mv = sb("mv", [P, KT, 2])
        gs = sb("gs", [P, 8, KT])
        expo = sb("expo", [P, KT])
        nmax = sb("nmax", [P, 4])
        rmax = sb("rmax", [P, 4])
        pspare = sb("pspare", [P, 4])
        spare = sb("spare", [P, 8])
        rsum = sb("rsum", [P, 2, GRP])
        rinv = sb("rinv", [P, 2, GRP])
        rb = sb("rb", [P, 2, HALF])

        sps = [ctx.enter_context(nc.psum_tensor(f"sps{i}", [P, N], F32)) for i in range(2)]
        tps = [ctx.enter_context(nc.psum_tensor(f"tps{i}", [P, HALF], F32)) for i in range(2)]
        ops = [ctx.enter_context(nc.psum_tensor(f"ops{i}", [P, HALF], F32)) for i in range(2)]

        BQ0, BK0, BV0, BP0, G0, BE0, BQ1, BK1, BV1, BP1, G1, BE1 = range(12)
        KB1, TWC, BO0, BO1 = range(4)
        ptv = pt[:].rearrange("p (l m n) -> p l m n", l=2, m=MT)
        wbig = [pt[:, i * 2 * KT * C:(i + 1) * 2 * KT * C].rearrange("p (l k n) -> p l k n", l=2, k=KT)
                for i in range(2)]
        pts = [[ptv[:, 0], ptv[:, 1]], [pb_hi[:], pb_lo[:]]]
        vpx = vp[:].rearrange("p m (x d) -> p m x d", x=4)
        v32x = v32[:].rearrange("p m (q e d) -> p m q e d", q=PAIRS, e=2)
        wqkf = wqk[:].rearrange("p l k n -> p (l k n)").bitcast(F32)
        wpf = wp[:].rearrange("p l n -> p (l n)").bitcast(F32)
        wvf = pt[:, 0:2 * KT * C].bitcast(F32)
        LOW, HIGH = slice(0, HD), slice(HD, P)
        own = (LOW, HIGH)
        other = (HIGH, LOW)

        s_ready = [sem("s_ready0"), sem("s_ready1")]
        s_free = [sem("s_free0"), sem("s_free1")]
        t_ready = [sem("t_ready0"), sem("t_ready1")]
        t_done = sem("t_done")
        hi_done = sem("hi_done")
        o_ready = [sem("o_ready0"), sem("o_ready1")]
        o_done = sem("o_done")
        raw_max = sem("raw_max")
        maxed = sem("maxed")
        inv_done = sem("inv_done")
        r_mid = sem("r_mid")
        r_in = sem("r_in")
        o_moved = sem("o_moved")
        rb_free = sem("rb_free")
        o3_hi = sem("o3_hi")
        o_hi = sem("o_hi")
        o_split = sem("o_split")
        o_scaled = sem("o_scaled")
        ev_hi = sem("ev_hi")
        first_head = sem("first_head")
        k_dup = sem("k_dup")
        vp_done = sem("vp_done")
        gn_step = sem("gn_step")
        gn_stat = sem("gn_stat")
        gn_pow = sem("gn_pow")
        gn_coef = sem("gn_coef")
        gn_val = sem("gn_val")
        gn_hi = sem("gn_hi")
        gn_lo = sem("gn_lo")
        x_in = sem("x_in")
        y_set = sem("y_set")
        wqk_in = sem("wqk_in")
        wp_in = sem("wp_in")
        wv_in = sem("wv_in")
        m_in = sem("m_in")
        y_out = sem("y_out")
        c_in = sem("c_in")
        WQ0, WK0, WV0, WP0, M1, M2 = range(6)
        w_in = [sem(f"{n}_in") for n in ("wq0", "wk0", "wv0", "wp0", "wk1_wq1", "wv1_wp1")]
        w_hi = [sem(f"{n}_hi") for n in ("wq0", "wk0", "wv0", "wp0", "m1", "m2")]
        w_lo = [sem(f"{n}_lo") for n in ("wq0", "wk0", "wv0", "wp0", "m1", "m2")]
        qk_out = sem("qk_out")
        w_out = sem("w_out")
        p_mm = sem("p_mm")
        p_vec = sem("p_vec")
        p_one = sem("p_one")

        def s_unit(b, u):
            return u % 2, b * (S_BATCH // 2) + u // 2

        def s_pair(b, p, j):
            return j % 2, b * (S_BATCH // 2) + p * (S_PAIR // 2) + (S_PRE + j) // 2

        def o_unit(b, u):
            return u % 2, b * (O_BATCH // 2) + 1 + u // 2

        def o_pair(b, p, u):
            return u % 2, b * (O_BATCH // 2) + p * (O_PAIR // 2) + (1 + u // 2)

        def o_pair_count(b, p, u):
            return b * O_BATCH + p * O_PAIR + (2 + u + 1 + 2)

        def o_count(b, u):
            return b * O_BATCH + 2 + u + 1 + 2

        block = ctx.enter_context(nc.Block())
        def halves(t):
            return [t[:, :, h * C:(h + 1) * C] for h in range(2)]

        def split_place(t):
            return t.rearrange("p (l k n) -> p l k n", l=2, k=KT)

        wk1_raw, wq1_raw = halves(y[:])
        wv1_raw, wp1_raw = halves(v32[:].rearrange("p m c -> p (m c)").rearrange("p (k n) -> p k n", k=KT))
        raw = {n: w_raw[:, n] for n in (WQ0, WK0, WV0, WP0)}
        split = {WQ0: split_place(kq[:, 0:4, :].rearrange("p a n -> p (a n)")),
                 WK0: split_place(kq[:, 4:8, :].rearrange("p a n -> p (a n)")),
                 WV0: wbig[0], M1: wbig[1],
                 WP0: split_place(pb_lo[:].rearrange("p m n -> p (m n)")),
                 M2: split_place(y[:].bitcast(F32R).rearrange("p k n -> p (k n)"))}
        scales = {WQ0: SCALE0, M1: SCALE1}
        QK_OUT, W_OUT = 2 * 16 * (PAIRS + 1), 16 * (PAIRS + 2)

        @block.sync
        def _(sp):
            def load(dst, w, n):
                sp.dma_start(dst, w.rearrange("(k p) n -> p k n", p=P)).then_inc(w_in[n], 16)

            load(wk1_raw, wk1, M1)
            load(wq1_raw, wq1, M1)
            for dst, a in ((vec, vectors), (idn, ident), (gm, gmean)):
                sp.dma_start(dst[:], a).then_inc(c_in, 16)
            sp.dma_start(xin[:], x[0]).then_inc(x_in, 16)
            load(raw[WQ0], wq0, WQ0)
            load(raw[WK0], wk0, WK0)
            load(raw[WP0], wp0, WP0)
            load(wv1_raw, wv1, M2)
            load(wp1_raw, wp1, M2)
            load(raw[WV0], wv0, WV0)
            for n in (WQ0, WK0):
                sp.wait_ge(w_lo[n], KT)
                src = split[n].bitcast(F32).rearrange("p l k n -> p (l k) n")
                cols = slice((n == WK0) * P, (n == WK0) * P + P)
                sp.dma_start(wqk[:].bitcast(F32).rearrange("p l k n -> p (l k) n")[:, :, cols],
                             src[:, :, 0:P]).then_inc(wqk_in, 16)
                for p in range(PAIRS + 1):
                    dst = WQK_D[p].rearrange("p (a n) -> p a n", a=2 * KT)
                    q = p % PAIRS
                    sp.dma_start(dst[:, :, cols], src[:, :, q * P:(q + 1) * P]).then_inc(qk_out, 16)

            def store_whole(n, dst, sem):
                sp.dma_start(dst, split[n].bitcast(F32).rearrange("p l k n -> p (l k n)")).then_inc(sem, 16)

            sp.wait_ge(w_lo[M1], KT)
            store_whole(M1, M1_D, w_out)
            sp.wait_ge(w_lo[WP0], KT)
            src = split[WP0].bitcast(F32)
            sp.dma_start(wp[:].bitcast(F32), src[:, :, 0, :]).then_inc(wp_in, 16)
            for p in range(PAIRS):
                sp.dma_start(WP_D[p].rearrange("p (l n) -> p l n", l=2), src[:, :, p, :]).then_inc(w_out, 16)
            sp.wait_ge(wv_in, 16)
            store_whole(WV0, WV_D, w_out)
            sp.wait_ge(w_lo[M2], KT - 2)
            for i in range(2):
                sp.wait_ge(s_free[i], 1)
            store_whole(M2, M2_D, y_out)
            sp.wait_ge(qk_out, QK_OUT)

            def spread_inverse(c, slot):
                sp.wait_ge(rb_free, c + 1)
                sp.wait_ge(inv_done, c + 1)
                sp.dma_start(R_D[slot].rearrange("g p -> p g"), rinv[:, slot, :],
                             allow_slow_non_contiguous=True).then_inc(r_mid, 16)
                sp.wait_ge(r_mid, 16 * (c + 1))
                src = R_D[slot].rearrange("g p -> (g p)").rearrange("(a n) -> a n", a=1)
                sp.dma_start(rb[:, slot, :], src.broadcast_to([P, HALF])).then_inc(r_in, 16)

            def after_qk(k_unit, q_unit, weights):
                sp.wait_ge(s_free[k_unit[0]], k_unit[1] + 2)
                for t in range(2, 6):
                    a, z = own[t % 2], other[t % 2]
                    sp.dma_start(kq[z, t, :].bitcast(F32), kq[a, t, :].bitcast(F32)).then_inc(k_dup, 16)
                sp.wait_ge(s_ready[q_unit[0]], q_unit[1] + 1)
                sp.dma_start(wqkf, weights).then_inc(wqk_in, 16)

            with sp.Fori(0, B) as b:
                following = sp.snap((b + 1) % B)
                after_qk(s_unit(b, 0), s_unit(b, 1), WQK_D[1])
                sp.wait_ge(w_out, W_OUT)
                sp.wait_ge(y_out, 16)
                with sp.Fori(0, PAIRS - 1) as p:
                    for g in range(4):
                        spread_inverse(b * R_BATCH + p * 4 + g, g % 2)
                    after_qk(s_pair(b, p, BLK), s_pair(b, p, BLK + 1), WQK_D[p + 2])
                    proj = o_pair(b, p, O_PAIR - 1)
                    sp.wait_ge(o_ready[proj[0]], proj[1] + 1)
                    sp.dma_start(wpf, WP_D[p + 1]).then_inc(wp_in, 16)
                for g in range(4):
                    spread_inverse(b * R_BATCH + 4 * (PAIRS - 1) + g, g % 2)
                pv = o_unit(b, (PAIRS - 1) * O_PAIR + 2)
                sp.wait_ge(o_ready[pv[0]], pv[1] + 1)
                sp.dma_start(pt[:, 0:2 * KT * C].bitcast(F32), M1_D).then_inc(m_in, 16)
                sp.dma_start(pt[:, 2 * KT * C:].bitcast(F32), M2_D).then_inc(m_in, 16)
                pv = o_unit(b, (PAIRS - 1) * O_PAIR + 3)
                sp.wait_ge(y_set, b * KT + KT)
                sp.wait_ge(o_ready[pv[0]], pv[1] + 1)
                sp.dma_start(xin[:], x[bass.ds(following, 1)].rearrange("b p k n -> (b p) k n")).then_inc(x_in, 16)
                proj = o_unit(b, O_GN1 - 1)
                sp.wait_ge(o_ready[proj[0]], proj[1] + 1)
                sp.dma_start(wpf, WP_D[0]).then_inc(wp_in, 16)
                for h in range(NH):
                    spread_inverse(b * R_BATCH + 4 * PAIRS + h, h)
                    for c in range(KT):
                        if h == NH - 1 and c == KT - 1:
                            bank, n = o_unit(b, O_BATCH - 1)
                            sp.wait_ge(o_ready[bank], n + 1)
                            sp.dma_start(wvf, WV_D).then_inc(wv_in, 16)
                        sp.wait_ge(o_done, o_count(b, O_PV1 + h * KT + c))
                        cols = slice(h * HALF, (h + 1) * HALF)
                        sp.dma_start(out[b, :, c, cols], y[:, c, cols]).then_inc(y_out, 16)
            sp.wait_ge(y_out, 16 + 16 * B * KT * NH)
            sp.wait_ge(wv_in, 16 * (B + 1))
            sp.wait_ge(x_in, 16 * (B + 1))
            sp.wait_ge(wqk_in, 16 * (B * PAIRS + 2))
            sp.wait_ge(wp_in, 16 * (B * PAIRS + 1))

        @block.tensor
        def _(pe):
            mm = nc.tensor.matmul
            def by_vector(dst, w, col):
                for c in range(KT):
                    for k in range(KT):
                        ins = mm(dst[:, c:c + 1], w[:, k, c * P:(c + 1) * P], vec[:, col, k:k + 1],
                                 start=k == 0, stop=k == KT - 1)
                return ins

            def product(left, right):
                for c in range(KT):
                    for k in range(KT):
                        ins = mm(sps[c // 2][:, c % 2 * HALF:(c % 2 + 1) * HALF],
                                 left[:, k, c * P:(c + 1) * P], right[:, k, :], start=k == 0, stop=k == KT - 1)
                    ins.then_inc(p_mm, 1)

            def s_take(unit):
                pe.wait_ge(s_free[unit[0]], unit[1] + 1)
                return sps[unit[0]]

            def split_mm(dst, left, right):
                n = len(left)
                for k in range(n):
                    for i, (a, w) in enumerate(((0, 0), (0, 1), (1, 0))):
                        ins = mm(dst, left[k][a], right[k][w], start=k == 0 and i == 0,
                                 stop=k == n - 1 and i == 2)
                return ins

            def cut(t, lo, hi):
                return [[t[:, l, k, lo:hi] for l in range(2)] for k in range(KT)]

            def gn_matmul(b, which, u, i):
                bank, n = o_unit(b, u + i)
                pe.wait_ge(o_done, o_count(b, u + i) - 2)
                pe.wait_ge(gn_stat, b * (2 * (KT + 1)) + which * (KT + 1) + KT + i)
                src = mv[:, :, 0] if i == 0 else gs[:, 1, :]
                mm(ops[bank][:, 0:KT], gm[:], src, start=True, stop=True).then_inc(o_ready[bank], 1)

            def two_halves(units, left, right, order):
                dsts = [s_take(unit) for unit in units]
                for n, k, arrival in order:
                    if arrival is not None:
                        pe.wait_ge(gn_lo, arrival)
                    for h in range(2):
                        for i, (a, w) in enumerate(((0, 0), (0, 1), (1, 0))):
                            last = mm(dsts[n][:, h * HALF:(h + 1) * HALF], left(n, h, k, a), right(h, k, w),
                                      start=k == 0 and i == 0, stop=k == KT - 1 and i == 2)
                    if k == KT - 1:
                        last.then_inc(s_ready[units[n][0]], 1)

            def v_units(b, first, w):
                for m in range(0, MT, 2):
                    two_halves([s_unit(b, first + m // 2)], lambda n, h, k, a: xn[:, a, k, (m + h) * P:(m + h + 1) * P],
                               lambda h, k, l: w[:, l, k, :], [(0, k, None) for k in range(KT)])

            def channel_units(units, w, los, order):
                two_halves(units, lambda n, h, k, a: w[:, a, k, los[n]:los[n] + P],
                           lambda h, k, l: xn[:, l, k, h * HALF:(h + 1) * HALF], order)

            def channel_unit(unit, w, lo, arrival=None):
                channel_units([unit], w, (lo,), [(0, k, None if arrival is None else arrival + k + 1)
                                                 for k in range(KT)])

            def scores0(unit, i):
                head, m = i // MT, i % MT
                dst = s_take(unit)
                for h in range(NH):
                    for l in range(2):
                        last = mm(dst[:, h * HALF:(h + 1) * HALF], kq[:, head, m * P:(m + 1) * P],
                                  kq[:, 2 + 2 * l + head, h * HALF:(h + 1) * HALF], start=l == 0, stop=l == 1)
                last.then_inc(s_ready[unit[0]], 1)

            def transposes(t, unit, i):
                pe.wait_ge(s_free[unit[0]], unit[1] + 2)
                for h in range(2):
                    pe.wait_ge(t_done, t + h + 1)
                    for j in range(4):
                        last = nc.tensor.transpose(tps[h][:, j * P:(j + 1) * P],
                                                   pr[:, i % 2, (4 * h + j) * P:(4 * h + j + 1) * P], idn[:])
                    last.then_inc(t_ready[h], 1)

            def pv0(b, p, g, tiles, blocks=range(GRP)):
                lo, hi = blocks[0] * P, blocks[-1] * P + P
                if tiles[0] == 0:
                    if g % 2 == 0:
                        pe.wait_ge(vp_done, b * HEADS + p * 2 + (g // 2 + 1))
                    pe.wait_ge(o_done, b * O_BATCH + p * O_PAIR + (2 + g + 1))
                    pe.wait_ge(t_done, b * T_BATCH + p * T_PAIR + (2 * (GRP * g + blocks[-1] + 1) + 2))
                head = g // 2
                for m in tiles:
                    for l in range(2):
                        last = mm(ops[g % 2][:, lo:hi], vp[:, m, head * P:(head + 1) * P],
                                  pts[g % 2][l][:, m, lo:hi],
                                  start=m == 0 and l == 0, stop=m == MT - 1 and l == 1)
                if tiles[-1] == MT - 1 and blocks[-1] == GRP - 1:
                    last.then_inc(o_ready[g % 2], 1)

            def projection(b, p, h):
                pe.wait_ge(o_split, b * G_BATCH + p * 4 + (h + 3 + 1))
                for c in range(KT):
                    u = 4 + h * KT + c
                    pe.wait_ge(o_done, o_pair_count(b, p, u) - 2)
                    split_mm(ops[u % 2][:], [[wp[:, l, c * P:(c + 1) * P] for l in range(2)]],
                             [[kq[:, 6 + l, h * HALF:(h + 1) * HALF] for l in range(2)]]).then_inc(o_ready[u % 2], 1)

            def pair(b, p, unit_of, more):
                for i in range(BLK):
                    if i + 2 < BLK:
                        scores0(unit_of(i + 2), i + 2)
                    transposes(b * T_BATCH + p * T_PAIR + 2 * i, unit_of(i), i)
                    if i >= GRP:
                        shares = (0, 3, 6, 8, 8) if i >= BLK - GRP else (0, 2, 4, 6, 8)
                        if shares[i % GRP] < shares[i % GRP + 1]:
                            pv0(b, p, i // GRP - 1, range(shares[i % GRP], shares[i % GRP + 1]))
                if more:
                    pe.wait_ge(wqk_in, b * (16 * PAIRS) + p * 16 + 48)
                    channel_unit(unit_of(BLK), wqk, P)
                    channel_unit(unit_of(BLK + 1), wqk, 0)
                    pv0(b, p, 3, range(MT))
                    pe.wait_ge(k_dup, b * (64 * PAIRS) + p * 64 + 128)
                    q_unit = unit_of(BLK + 1)
                    pe.wait_ge(s_free[q_unit[0]], q_unit[1] + 2)
                    scores0(unit_of(BLK + 2), 0)
                    scores0(unit_of(BLK + 3), 1)
                else:
                    pv0(b, p, 3, range(MT), range(GRP // 2))
                    pv0(b, p, 3, range(MT), range(GRP // 2, GRP))
                pe.wait_ge(wp_in, b * (16 * PAIRS) + p * 16 + 16)
                projection(b, p, 0)
                projection(b, p, 1)

            pe.wait_ge(w_in[M1], 32)
            product(wk1_raw, wq1_raw)
            pe.wait_ge(c_in, 16 * 3)
            gn_matmul(0, 0, -2, 0)
            pe.wait_ge(p_vec, 1)
            pe.wait_ge(p_one, 1)
            by_vector(tps[0][:, 0:KT], wq1_raw, BK1)
            by_vector(tps[0][:, KT:2 * KT], wk1_raw, BQ1)
            for k in range(KT):
                last = mm(tps[0][:, 2 * KT:2 * KT + 1], ones[:], bb[:, k:k + 1], start=k == 0, stop=k == KT - 1)
            last.then_inc(p_mm, 1)
            gn_matmul(0, 0, -2, 1)
            pe.wait_ge(w_in[WP0], 16)
            by_vector(tps[1][:, 0:KT], raw[WP0], BV0).then_inc(p_mm, 1)
            pe.wait_ge(w_in[M2], 32)
            pe.wait_ge(w_lo[M1], KT)
            product(wv1_raw, wp1_raw)
            pe.wait_ge(p_vec, 6 + 2 * KT)
            by_vector(tps[0][:, 0:KT], wp1_raw, BV1).then_inc(p_mm, 1)
            with pe.Fori(0, B) as b:
                pe.wait_ge(p_vec, 7 + 2 * KT)
                pe.wait_ge(wqk_in, b * (16 * PAIRS) + 32)
                channel_unit(s_unit(b, 0), wqk, P, b * (2 * KT))
                channel_unit(s_unit(b, 1), wqk, 0)
                pe.wait_ge(wv_in, b * 16 + 16)
                v_units(b, 2, wbig[0])
                pe.wait_ge(k_dup, b * (64 * PAIRS) + 64)
                scores0(s_unit(b, S_PRE), 0)
                scores0(s_unit(b, S_PRE + 1), 1)
                with pe.Fori(0, PAIRS - 1) as p:
                    pair(b, p, lambda j: s_pair(b, p, j), True)
                pair(b, PAIRS - 1, lambda j: s_unit(b, S_PRE + (PAIRS - 1) * S_PAIR + j), False)

                gn_matmul(b, 1, O_GN1, 0)
                gn_matmul(b, 1, O_GN1, 1)
                pe.wait_ge(m_in, b * 32 + 32)
                arrival = b * (2 * KT) + KT
                channel_units([s_unit(b, S_POST), s_unit(b, S_POST + 1)], wbig[0], (0, P),
                              [(0, 0, arrival + 1), (1, 0, None), (0, 1, arrival + 2), (1, 1, None),
                               (0, 2, arrival + 3), (0, 3, arrival + 4), (1, 2, None), (1, 3, None)])
                for c in range(2, KT):
                    channel_unit(s_unit(b, S_POST + c), wbig[0], c * P)
                for h in range(NH):
                    pe.wait_ge(t_done, b * T_BATCH + (T_POST + h + 1))
                    split_mm(tps[h][:], cut(tw, 0, P), cut(xn, h * HALF, (h + 1) * HALF)).then_inc(t_ready[h], 1)
                v_units(b, S_POST + KT, wbig[1])

                def scores1(i):
                    unit = s_unit(b, S_POST + KT + MT // 2 + i)
                    dst = s_take(unit)
                    for h in range(NH):
                        last = split_mm(dst[:, h * HALF:(h + 1) * HALF], cut(xn, i * P, (i + 1) * P),
                                        [[kq[:, l * KT + k, h * HALF:(h + 1) * HALF] for l in range(2)]
                                         for k in range(KT)])
                    last.then_inc(s_ready[unit[0]], 1)

                def pv1(h, c, blocks=range(GRP)):
                    pe.wait_ge(t_done, b * T_BATCH + (T_POST + 2 + 2 * (GRP * h + blocks[-1] + 1) + 2))
                    bank, n = o_unit(b, O_PV1 + h * KT + c)
                    if blocks[0] == 0:
                        pe.wait_ge(o_done, o_count(b, O_PV1 + h * KT + c) - 2)
                    lo, hi = blocks[0] * P, blocks[-1] * P + P
                    last = split_mm(ops[bank][:, lo:hi],
                                    [[v[:, m, l * C + c * P:l * C + (c + 1) * P] for l in range(2)] for m in range(MT)],
                                    [[ptv[:, l, m, lo:hi] for l in range(2)] for m in range(MT)])
                    if blocks[-1] == GRP - 1:
                        last.then_inc(o_ready[bank], 1)

                scores1(0)
                scores1(1)
                for i in range(MT):
                    if i == GRP:
                        gn_matmul(b, 2, O_GN0, 1)
                        for c in range(KT):
                            pv1(0, c)
                    transposes(b * T_BATCH + (T_POST + 2 + 2 * i), s_unit(b, S_POST + KT + MT // 2 + i), i)
                    if i == GRP - 1:
                        gn_matmul(b, 2, O_GN0, 0)
                    if i + 2 < MT:
                        scores1(i + 2)
                    else:
                        pv1(1, i + 2 - MT, range(GRP // 2))
                pv1(1, 0, range(GRP // 2, GRP))
                pv1(1, 1, range(GRP // 2, GRP))
                pv1(1, 2)
                pv1(1, 3)

        @block.scalar
        def _(act):
            def hi_of(dst, src, bias, sem, scale=1.0):
                nc.scalar.activation(dst, src, ACT.Identity, bias=bias, scale=scale).then_inc(sem, 1)

            def group_norm(b, src, which):
                act.wait_ge(gn_coef, b * 2 + (which + 1))
                for k in range(KT):
                    hi_of(xn[:, 0, k, :], src[:, k, :], gs[:, 3, k:k + 1], gn_hi, gs[:, 6, k:k + 1])

            def filled(unit):
                act.wait_ge(s_ready[unit[0]], unit[1] + 1)
                return sps[unit[0]]

            def exp(i, m, unit, free):
                act.wait_ge(maxed, m + 1)
                if free is not None:
                    act.wait_ge(t_ready[1], free)
                nc.scalar.activation(pr[:, i % 2, :], sps[unit[0]][:], ACT.Exp, bias=nmax[:, i % 4:i % 4 + 1],
                                     accum_out=rsum[:, i // GRP % 2, i % GRP:i % GRP + 1]).then_inc(s_free[unit[0]], 1)

            def p_hi(t, i, buf):
                for h in range(2):
                    act.wait_ge(t_ready[h], t + 1)
                    dst = pts[buf][0][:, 4 * h:4 * h + 4, i % GRP * P:(i % GRP + 1) * P]
                    nc.scalar.activation(dst, tps[h][:].rearrange("p (m n) -> p m n", m=4),
                                         ACT.Identity, bias=0.0).then_inc(hi_done, 1)

            def move(b, p, g):
                e = g // 2
                act.wait_ge(o_ready[g % 2], b * (O_BATCH // 2) + p * (O_PAIR // 2) + (1 + g // 2 + 1))
                act.wait_ge(o_done, b * O_BATCH + p * O_PAIR + (2 + g + 2))
                nc.scalar.activation(otmp[own[e], :], ops[g % 2][other[e], :], ACT.Identity,
                                     bias=0.0).then_inc(o_moved, 1)

            def v_hi(p, e):
                src = v32x[:, :, p, e] if isinstance(p, int) else v32[:, :, bass.ds(p * 2 * HD + e * HD, HD)]
                nc.scalar.activation(vpx[:, :, 3 * e, :], src, ACT.Identity, bias=0.0).then_inc(ev_hi, 1)

            def qk_hi(unit, slot, col, p):
                src = filled(unit)
                for e in range(2):
                    bias = vec[own[e], col, p:p + 1] if isinstance(p, int) else vec[own[e], col, bass.ds(p, 1)]
                    hi_of(kq[own[e], slot + e, :], src[own[e], :], bias, ev_hi)

            def pair(b, p, unit_of, more):
                tn = b * (T_BATCH // 2) + p * BLK
                m = b * M_BATCH + p * BLK
                exp(0, m, unit_of(0), None)
                exp(1, m + 1, unit_of(1), None)
                for i in range(BLK):
                    g = i // GRP
                    if i % GRP == 0:
                        act.wait_ge(o_ready[g % 2], b * (O_BATCH // 2) + p * (O_PAIR // 2) + (1 + g // 2))
                    if i == GRP:
                        act.wait_ge(y_set, b * KT + KT)
                    if i == BLK - 1:
                        move(b, p, 2)
                    p_hi(tn + i, i, g % 2)
                    if i + 2 < BLK:
                        exp(i + 2, m + i + 2, unit_of(i + 2), tn + i + 1)
                    if i >= 2 * GRP and i % GRP == 0:
                        move(b, p, g - 2)
                    if i in (0, GRP):
                        v_hi(p, i // GRP)
                if more:
                    qk_hi(unit_of(BLK), 2, BK0, p + 1)
                    qk_hi(unit_of(BLK + 1), 0, BQ0, p + 1)
                move(b, p, 3)
                act.wait_ge(rb_free, b * R_BATCH + p * 4 + (3 + 3))
                cols = slice(HALF, 2 * HALF)
                nc.scalar.activation(kq[own[1], 6, cols], osum[own[1], :], ACT.Identity, bias=0.0).then_inc(o3_hi, 1)

            def merged_hi(n, done, k):
                act.wait_ge(p_mm, done + k + 1)
                nc.scalar.activation(split[n][:, 0, k, :], sps[k // 2][:, k % 2 * HALF:(k % 2 + 1) * HALF],
                                     ACT.Identity, bias=0.0, scale=scales.get(n, 1.0)).then_inc(w_hi[n], 1)

            for k in range(KT):
                if k == 0:
                    act.wait_ge(c_in, 16 * 3)
                merged_hi(M1, 0, k)
            act.wait_ge(x_in, 16)
            act.wait_ge(gn_coef, 1)
            for k in range(KT):
                hi_of(xn[:, 0, k, :], xin[:, k, :], gs[:, 3, k:k + 1], gn_hi, gs[:, 6, k:k + 1])
                if k % 2 == 1:
                    merged_hi(M2, KT + 2, k - 1)
                    merged_hi(M2, KT + 2, k)
            act.wait_ge(qk_out, QK_OUT)
            act.wait_ge(wqk_in, 32)
            with act.Fori(0, B) as b:
                qk_hi(s_unit(b, 0), 2, BK0, 0)
                qk_hi(s_unit(b, 1), 0, BQ0, 0)
                for u in range(MT // 2):
                    unit = s_unit(b, 2 + u)
                    src = filled(unit)
                    nc.scalar.activation(v32[:, 2 * u:2 * u + 2, :], src[:].rearrange("p (m c) -> p m c", m=2),
                                         ACT.Identity, bias=0.0).then_inc(s_free[unit[0]], 1)
                    if u == 0:
                        act.wait_ge(y_out, b * (16 * KT * NH) + 16)
                    nc.scalar.activation(y[:, u, :], xin[:, u, :], ACT.Identity,
                                         bias=der[:, BO0, u:u + 1]).then_inc(y_set, 1)
                act.wait_ge(w_out, W_OUT)
                act.wait_ge(wp_in, 16)
                for u in range(S_PRE - 2, S_PRE):
                    unit = s_unit(b, u)
                    act.wait_ge(s_free[unit[0]], unit[1] + 2)
                with act.Fori(0, PAIRS - 1) as p:
                    pair(b, p, lambda j: s_pair(b, p, j), True)
                pair(b, PAIRS - 1, lambda j: s_unit(b, S_PRE + (PAIRS - 1) * S_PAIR + j), False)

                group_norm(b, y, 1)
                for c in range(KT):
                    hi_of(kq[:, c, :], filled(s_unit(b, S_POST + c))[:], der[:, KB1, c:c + 1], ev_hi)
                for u in range(MT // 2):
                    src = filled(s_unit(b, S_POST + KT + u))
                    nc.scalar.activation(v[:, 2 * u:2 * u + 2, 0:C], src[:].rearrange("p (m c) -> p m c", m=2),
                                         ACT.Identity, bias=0.0).then_inc(ev_hi, 1)
                first = S_POST + KT + MT // 2
                tn = b * (T_BATCH // 2) + (T_POST // 2 + 1)
                m = b * M_BATCH + PAIRS * BLK
                exp(0, m, s_unit(b, first), None)
                exp(1, m + 1, s_unit(b, first + 1), None)
                for i in range(MT):
                    if i == GRP:
                        bank, n = o_unit(b, O_PV1 + KT - 1)
                        act.wait_ge(o_ready[bank], n + 1)
                    p_hi(tn + i, i, 0)
                    if i + 2 < MT:
                        exp(i + 2, m + i + 2, s_unit(b, first + i + 2), tn + i + 1)
                group_norm(b, xin, 2)

        @block.vector
        def _(dve):
            op = nc.vector
            op.memset(ones[:], 1.0).then_inc(p_one, 1)
            op.memset(expo[:], -0.5).then_inc(p_one, 1)
            for n, s in enumerate((t_done, t_done, o_done, o_done)):
                op.memset(spare[:, n:n + 1], 0.0).then_inc(s, 1)
            dve.wait_ge(c_in, 16 * 3)
            dve.wait_ge(p_one, 2)
            op.tensor_tensor(bb[:], vec[:, BQ1, :], vec[:, BK1, :], ALU.mult).then_inc(p_vec, 1)
            op.tensor_scalar(vec[:, BQ0, :], vec[:, BQ0, :], SCALE0, None, ALU.mult).then_inc(p_vec, 1)

            def lo_part(n, k, src, sem, by=1):
                dve.wait_ge(w_hi[n], k + 1)
                op.scalar_tensor_tensor(out=split[n][:, 1, k, :], in0=src, scalar=scales.get(n, 1.0),
                                        in1=split[n][:, 0, k, :].bitcast(F32), op0=ALU.mult,
                                        op1=ALU.subtract).then_inc(sem, by)

            def split_weight(n):
                dve.wait_ge(w_in[n], 16)
                for k in range(KT):
                    op.tensor_scalar(split[n][:, 0, k, :], raw[n][:, k, :], scales.get(n, 1.0), None,
                                     ALU.mult).then_inc(w_hi[n], 1)
                    if n == WV0:
                        lo_part(n, k, raw[n][:, k, :], wv_in, 16 // KT)
                    else:
                        lo_part(n, k, raw[n][:, k, :], w_lo[n])

            def split_merged(n, ks):
                for k in ks:
                    lo_part(n, k, sps[k // 2][:, k % 2 * HALF:(k % 2 + 1) * HALF],
                            s_free[k // 2] if n == M2 and k % 2 == 1 else w_lo[n])

            def bias_terms():
                dve.wait_ge(p_mm, KT + 1)
                op.tensor_scalar(der[:, KB1, :], tps[0][:, 0:KT], SCALE1, None, ALU.mult).then_inc(p_vec, 1)
                op.tensor_scalar(der[:, TWC, :], tps[0][:, KT:2 * KT], SCALE1, None, ALU.mult).then_inc(p_vec, 1)
                op.tensor_scalar(t0[:], tps[0][:, 2 * KT:2 * KT + 1], SCALE1, None, ALU.mult).then_inc(p_vec, 1)
                dve.wait_ge(p_vec, 5)
                for k in range(KT):
                    op.tensor_scalar(tw[:, 0, k, :], ones[:], der[:, TWC, k:k + 1], None, ALU.mult).then_inc(p_vec, 1)
                dve.wait_ge(p_vec, 5 + KT)
                for k in range(KT):
                    op.scalar_tensor_tensor(out=tw[:, 1, k, :], in0=ones[:], scalar=der[:, TWC, k:k + 1],
                                            in1=tw[:, 0, k, :].bitcast(F32), op0=ALU.mult,
                                            op1=ALU.subtract).then_inc(p_vec, 1)

            def filled(unit):
                dve.wait_ge(s_ready[unit[0]], unit[1] + 1)
                return sps[unit[0]]

            def gn_stats(src, k, h):
                op.bn_stats(bst[:, k, h, :], src[:, k, h * HALF:(h + 1) * HALF]).then_inc(gn_step, 1)

            def gn_mean(b, which):
                dve.wait_ge(gn_step, b * (2 * GN_STEPS) + (which * GN_STEPS + NH * KT))
                op.memset(spare[:, 6:7], 0.0)
                for k in range(KT):
                    op.bn_aggr(mv[:, k, :], bst[:, k, :, :].rearrange("p h s -> p (h s)")).then_inc(gn_stat, 1)

            def gn_deviation(b, which, u):
                step0 = b * (2 * GN_STEPS) + (which * GN_STEPS + NH * KT)
                dve.wait_ge(gn_stat, b * (2 * (KT + 1)) + (which * (KT + 1) + KT))
                bank, n = o_unit(b, u)
                dve.wait_ge(o_ready[bank], n + 1)
                op.tensor_tensor(gs[:, 0, :], mv[:, :, 0], ops[bank][:, 0:KT], ALU.subtract).then_inc(gn_step, 1)
                op.tensor_copy(gs[:, 2, :], ops[bank][:, 0:KT]).then_inc(o_done, 1)
                dve.wait_ge(gn_step, step0 + 1)
                op.tensor_tensor(gs[:, 4, :], gs[:, 0, :], gs[:, 0, :], ALU.mult).then_inc(gn_step, 1)
                dve.wait_ge(gn_step, step0 + 2)
                op.tensor_tensor(gs[:, 1, :], gs[:, 4, :], mv[:, :, 1], ALU.add).then_inc(gn_stat, 1)

            def gn_variance(b, u, eps):
                bank, n = o_unit(b, u + 1)
                dve.wait_ge(o_ready[bank], n + 1)
                op.tensor_scalar(gs[:, 5, :], ops[bank][:, 0:KT], eps, None, ALU.add).then_inc(o_done, 1)

            def gn_coefficients(b, which, u, gamma, beta):
                step0 = b * (2 * GN_STEPS) + (which * GN_STEPS + NH * KT)
                dve.wait_ge(gn_pow, b * 2 + (which + 1))
                op.tensor_tensor(gs[:, 6, :], gs[:, 7, :], vec[:, gamma, :], ALU.mult).then_inc(gn_step, 1)
                dve.wait_ge(o_done, o_count(b, u))
                dve.wait_ge(gn_step, step0 + 3)
                op.tensor_tensor(gs[:, 4, :], gs[:, 2, :], gs[:, 6, :], ALU.mult).then_inc(gn_step, 1)
                dve.wait_ge(gn_step, step0 + 4)
                op.tensor_tensor(gs[:, 3, :], vec[:, beta, :], gs[:, 4, :], ALU.subtract).then_inc(gn_coef, 1)
                dve.wait_ge(gn_coef, b * 2 + (which + 1))

            def gn_apply(b, which, src, k):
                done = b * (2 * KT) + (which * KT + k)
                if k >= 2:
                    dve.wait_ge(gn_lo, done - 1)
                op.tensor_scalar(pr[:, k % 2, :], src[:, k, :], gs[:, 6, k:k + 1], gs[:, 3, k:k + 1],
                                 ALU.mult, ALU.add).then_inc(gn_val, 1)
                dve.wait_ge(gn_val, done + 1)
                dve.wait_ge(gn_hi, done + 1)
                op.tensor_tensor(xn[:, 1, k, :], pr[:, k % 2, :], xn[:, 0, k, :].bitcast(F32),
                                 ALU.subtract).then_inc(gn_lo, 1)

            def lo_of(dst, src, bias, hi, sem):
                op.scalar_tensor_tensor(out=dst, in0=src, scalar=bias, in1=hi.bitcast(F32), op0=ALU.add,
                                        op1=ALU.subtract).then_inc(sem, 1)

            def vec_of(col, e, p):
                return vec[own[e], col, p:p + 1] if isinstance(p, int) else vec[own[e], col, bass.ds(p, 1)]

            def k_lo(unit, e0, p):
                src = filled(unit)
                for e in range(2):
                    dve.wait_ge(ev_hi, e0 + e + 1)
                    lo_of(kq[own[e], 4 + e, :], src[own[e], :], vec_of(BK0, e, p), kq[own[e], 2 + e, :],
                          s_free[unit[0]] if e else first_head)

            def q_lo(unit, e0, p):
                src = filled(unit)
                for e in range(2):
                    dve.wait_ge(ev_hi, e0 + e + 1)
                    lo_of(kq[other[e], e, :], src[own[e], :], vec_of(BQ0, e, p), kq[own[e], e, :],
                          s_free[unit[0]] if e else first_head)

            def v_lo(e0, p, e):
                src = v32x[:, :, p, e] if isinstance(p, int) else v32[:, :, bass.ds(p * 2 * HD + e * HD, HD)]
                dve.wait_ge(ev_hi, e0 + 1)
                op.tensor_tensor(vpx[:, :, 1 + e, :], src, vpx[:, :, 3 * e, :].bitcast(F32),
                                 ALU.subtract).then_inc(vp_done, 1)

            def row_max(unit, m, i):
                src = filled(unit)
                op.tensor_reduce(out=nmax[:, i % 4:i % 4 + 1], in_=src[:], axis=AX.X, op=ALU.max,
                                 negate=True).then_inc(maxed, 1)

            def p_lo_part(m, i, buf):
                for h in range(2):
                    dve.wait_ge(hi_done, m * 2 + h + 1)
                    cols = slice(i % GRP * P, (i % GRP + 1) * P)
                    hi, lo = (t[:, 4 * h:4 * h + 4, cols] for t in pts[buf])
                    op.tensor_tensor(lo, tps[h][:].rearrange("p (m n) -> p m n", m=4), hi.bitcast(F32),
                                     ALU.subtract).then_inc(t_done, 1)

            def inverse(unit, i, sent=None):
                if sent is not None:
                    dve.wait_ge(r_mid, sent)
                dve.wait_ge(s_free[unit[0]], unit[1] + 2)
                slot = i // GRP % 2
                op.reciprocal(rinv[:, slot, :], rsum[:, slot, :]).then_inc(inv_done, 1)

            def joined(b, p, g):
                e = g // 2
                c = b * G_BATCH + p * 4 + g
                dve.wait_ge(o_moved, c + 1)
                dve.wait_ge(o_split, c + 1)
                op.tensor_tensor(osum[own[e], :], ops[g % 2][own[e], :], otmp[own[e], :], ALU.add).then_inc(o_done, 1)

            def add_projection(b, p, h, c):
                bank, n = o_pair(b, p, 4 + h * KT + c)
                there = y[:, c, h * HALF:(h + 1) * HALF]
                dve.wait_ge(o_ready[bank], n + 1)
                op.tensor_tensor(there, ops[bank][:], there, ALU.add).then_inc(o_done, 1)

            def added_stats(b, p, h, c):
                dve.wait_ge(o_done, o_pair_count(b, p, 4 + h * KT + c))
                gn_stats(y, c, h)

            def pair(b, p, unit_of, more):
                m = b * M_BATCH + p * BLK
                for i in range(BLK):
                    if i + 2 < BLK:
                        row_max(unit_of(i + 2), m + i + 2, i + 2)
                    if i > 2 * GRP and i % GRP == 1:
                        joined(b, p, i // GRP - 2)
                    if i == BLK - 1:
                        joined(b, p, 2)
                    if i in (1, GRP + 1):
                        v_lo(b * E_BATCH + p * E_PAIR + (E_PRE + i // GRP), p, i // GRP)
                    if i % GRP == GRP - 1:
                        g = i // GRP
                        inverse(unit_of(i), i, b * (16 * R_BATCH) + p * 64 + 16 * (g - 1) if g >= 2 else None)
                    p_lo_part(m + i, i, i // GRP % 2)
                dve.wait_ge(y_set, b * KT + KT)
                e0 = b * E_BATCH + p * E_PAIR + (E_PRE + 2)
                if more:
                    k_lo(unit_of(BLK), e0, p + 1)
                    q_lo(unit_of(BLK + 1), e0 + 2, p + 1)
                joined(b, p, 3)
                w, cols = own[1], slice(HALF, 2 * HALF)
                dve.wait_ge(o_done, b * O_BATCH + p * O_PAIR + (2 + 3 + 3))
                dve.wait_ge(r_in, b * (16 * R_BATCH) + p * 64 + 64)
                op.tensor_tensor(osum[w, :], osum[w, :], rb[w, 1, :], ALU.mult).then_inc(rb_free, 1)
                if more:
                    row_max(unit_of(BLK + 2), m + BLK, 0)
                else:
                    add_projection(b, p, 0, 0)
                dve.wait_ge(rb_free, b * R_BATCH + p * 4 + (3 + 3))
                dve.wait_ge(o3_hi, b * PAIRS + p + 1)
                op.tensor_tensor(kq[w, 7, cols], osum[w, :], kq[w, 6, cols].bitcast(F32), ALU.subtract).then_inc(o_split, 1)
                if more:
                    add_projection(b, p, 0, 0)
                for c in range(1, KT):
                    add_projection(b, p, 0, c)
                    if more and c == 1:
                        row_max(unit_of(BLK + 3), m + BLK + 1, 1)
                for c in range(KT):
                    add_projection(b, p, 1, c)
                    if not more and c > 0:
                        added_stats(b, p, 0, c - 1)
                if not more:
                    added_stats(b, p, 0, KT - 1)
                    for c in range(KT):
                        added_stats(b, p, 1, c)

            dve.wait_ge(x_in, 16)
            for k in range(KT):
                for h in range(NH):
                    gn_stats(xin, k, h)
            gn_mean(0, 0)
            split_weight(WQ0)
            split_weight(WK0)
            split_merged(M1, range(KT))
            gn_deviation(0, 0, -2)
            split_weight(WP0)
            split_weight(WV0)
            bias_terms()
            gn_variance(0, -2, EPS0)
            dve.wait_ge(p_mm, KT + 2)
            op.tensor_tensor(der[:, BO0, :], tps[1][:, 0:KT], vec[:, BP0, :], ALU.add).then_inc(p_vec, 1)
            dve.wait_ge(p_vec, 6 + 2 * KT)
            for n in (WQ0, WK0, WP0):
                dve.wait_ge(w_lo[n], KT)
            dve.wait_ge(wv_in, 16)
            gn_coefficients(0, 0, -2, G0, BE0)
            for k in range(KT):
                gn_apply(0, 0, xin, k)
                if k % 2 == 1:
                    split_merged(M2, (k - 1, k))
            dve.wait_ge(p_mm, 2 * KT + 3)
            op.tensor_tensor(der[:, BO1, :], tps[0][:, 0:KT], vec[:, BP1, :], ALU.add).then_inc(p_vec, 1)
            with dve.Fori(0, B) as b:
                k_lo(s_unit(b, 0), b * E_BATCH, 0)
                q_lo(s_unit(b, 1), b * E_BATCH + 2, 0)
                row_max(s_unit(b, S_PRE), b * M_BATCH, 0)
                row_max(s_unit(b, S_PRE + 1), b * M_BATCH + 1, 1)
                with dve.Fori(0, PAIRS - 1) as p:
                    pair(b, p, lambda j: s_pair(b, p, j), True)
                pair(b, PAIRS - 1, lambda j: s_unit(b, S_PRE + (PAIRS - 1) * S_PAIR + j), False)

                gn_mean(b, 1)
                gn_deviation(b, 1, O_GN1)
                gn_variance(b, O_GN1, EPS1)
                gn_coefficients(b, 1, O_GN1, G1, BE1)
                for k in range(KT):
                    gn_apply(b, 1, y, k)
                for c in range(KT):
                    unit = s_unit(b, S_POST + c)
                    src = filled(unit)
                    dve.wait_ge(ev_hi, b * E_BATCH + (E_K1 + c + 1))
                    lo_of(kq[:, KT + c, :], src[:], der[:, KB1, c:c + 1], kq[:, c, :], s_free[unit[0]])
                for h in range(NH):
                    dve.wait_ge(t_ready[h], b * (T_BATCH // 2) + (T_POST // 2 + 1))
                    op.tensor_scalar(trow[:, h * HALF:(h + 1) * HALF], tps[h][:], t0[:], None, ALU.add).then_inc(t_done, 1)
                for u in range(MT // 2):
                    unit = s_unit(b, S_POST + KT + u)
                    src = filled(unit)
                    dve.wait_ge(ev_hi, b * E_BATCH + (E_V1 + u + 1))
                    op.tensor_tensor(v[:, 2 * u:2 * u + 2, C:], src[:].rearrange("p (m c) -> p m c", m=2),
                                     v[:, 2 * u:2 * u + 2, 0:C].bitcast(F32), ALU.subtract).then_inc(s_free[unit[0]], 1)
                dve.wait_ge(t_done, b * T_BATCH + (T_POST + 2 + 2))
                m = b * M_BATCH + PAIRS * BLK

                def row_max1(i):
                    unit = s_unit(b, S_POST + KT + MT // 2 + i)
                    src = filled(unit)
                    op.memset(spare[:, 7:8], 0.0)
                    op.tensor_tensor_reduce(out=src[:], in0=src[:], in1=trow[:], scale=1.0, scalar=LOWEST,
                                            op0=ALU.add, op1=ALU.max,
                                            accum_out=rmax[:, i % 4:i % 4 + 1]).then_inc(raw_max, 1)
                    dve.wait_ge(raw_max, b * MT + i + 1)
                    op.tensor_scalar(nmax[:, i % 4:i % 4 + 1], rmax[:, i % 4:i % 4 + 1], -1.0, None,
                                     ALU.mult).then_inc(maxed, 1)

                def residual(h, c):
                    if c == 0:
                        dve.wait_ge(r_in, b * (16 * R_BATCH) + 16 * (4 * PAIRS + h + 1))
                    u = O_PV1 + h * KT + c
                    bank, n = o_unit(b, u)
                    cols = slice(h * HALF, (h + 1) * HALF)
                    dve.wait_ge(o_ready[bank], n + 1)
                    op.tensor_tensor(osum[:], ops[bank][:], rb[:, h, :], ALU.mult).then_inc(o_scaled, 1)
                    dve.wait_ge(o_scaled, b * (NH * KT) + (h * KT + c + 1))
                    op.scalar_tensor_tensor(out=y[:, c, cols], in0=osum[:], scalar=der[:, BO1, c:c + 1],
                                            in1=y[:, c, cols], op0=ALU.add, op1=ALU.add).then_inc(o_done, 1)
                    dve.wait_ge(o_done, o_count(b, u))
                    if c == KT - 1:
                        op.memset(spare[:, 0:1], 0.0).then_inc(rb_free, 1)

                row_max1(0)
                row_max1(1)
                for i in range(MT):
                    if i == 1:
                        dve.wait_ge(x_in, b * 16 + 32)
                    if i in (1, 2):
                        for k in (2 * i - 2, 2 * i - 1):
                            for h in range(NH):
                                gn_stats(xin, k, h)
                    if i == GRP - 1:
                        gn_mean(b, 2)
                    if i == GRP:
                        gn_variance(b, O_GN0, EPS0)
                        for c in range(KT):
                            residual(0, c)
                    if i == GRP + 1:
                        gn_coefficients(b, 2, O_GN0, G0, BE0)
                    if i % GRP == GRP - 1:
                        inverse(s_unit(b, S_POST + KT + MT // 2 + i), i)
                    p_lo_part(m + i, i, 0)
                    if i == GRP - 1:
                        gn_deviation(b, 2, O_GN0)
                    if i + 2 < MT:
                        row_max1(i + 2)
                gn_apply(b, 2, xin, 0)
                gn_apply(b, 2, xin, 1)
                residual(1, 0)
                gn_apply(b, 2, xin, 2)
                residual(1, 1)
                gn_apply(b, 2, xin, 3)
                residual(1, 2)
                residual(1, 3)

        @block.gpsimd
        def _(pool):
            op = nc.gpsimd

            def group_norm(b, u):
                pool.wait_ge(o_done, o_count(b, u + 1))
                op.tensor_tensor(gs[:, 7, :], gs[:, 5, :], expo[:], ALU.pow).then_inc(gn_pow, 1)

            def pair(b, p):
                for g in range(3):
                    c = b * (3 * PAIRS) + p * 3 + g
                    w = own[g // 2]
                    cols = slice(g % 2 * HALF, (g % 2 + 1) * HALF)
                    pool.wait_ge(o_done, b * O_BATCH + p * O_PAIR + (2 + g + 3))
                    pool.wait_ge(r_in, b * (16 * R_BATCH) + p * 64 + 16 * (g + 1))
                    op.tensor_tensor(kq[w, 6, cols], osum[w, :], rb[w, g % 2, :], ALU.mult).then_inc(o_hi, 1)
                    pool.wait_ge(o_hi, c + 1)
                    op.tensor_tensor(osum[w, :], osum[w, :], rb[w, g % 2, :], ALU.mult).then_inc(rb_free, 1)
                    pool.wait_ge(rb_free, b * R_BATCH + p * 4 + (g + 3))
                    op.tensor_tensor(kq[w, 7, cols], osum[w, :], kq[w, 6, cols].bitcast(F32),
                                     ALU.subtract).then_inc(o_split, 1)

            pool.wait_ge(p_one, 2)
            for n, s in enumerate((o_split, rb_free, rb_free)):
                op.memset(pspare[:, n:n + 1], 0.0).then_inc(s, 1)
            group_norm(0, -2)
            with pool.Fori(0, B) as b:
                with pool.Fori(0, PAIRS) as p:
                    pair(b, p)
                group_norm(b, O_GN1)
                group_norm(b, O_GN0)

    return nc


def kernel(**inputs):
    import numpy as _np
    import concourse.bacc as _bacc
    from concourse import mybir as _mybir
    from concourse.bass_utils import run_bass_kernel_spmd as _run

    def arr(name):
        return _np.asarray(inputs[name])

    def column(a):
        return _np.ascontiguousarray(a.reshape(-1, P).T)

    wqkv, bqkv = arr("L0_conv_w_qkv"), arr("L0_conv_b_qkv")
    xl = arr("x").reshape(B, KT, P, N).transpose(0, 2, 1, 3)
    gmean = _np.kron(_np.eye(P * GROUPS // C), _np.full((C // GROUPS,) * 2, GROUPS / C)).astype(_np.float32)
    vectors = [bqkv[0:C], bqkv[C:2 * C], bqkv[2 * C:]] + [arr(n) for n in (
        "L0_conv_b_proj", "L0_conv_gamma", "L0_conv_beta", "L1_conv_q_b", "L1_conv_k_b", "L1_conv_v_b",
        "L1_conv_proj_b", "L1_conv_gn_gamma", "L1_conv_gn_beta")]
    given = dict(
        x=xl, wq0=wqkv[0:C].T, wk0=wqkv[C:2 * C].T, wv0=wqkv[2 * C:].T, wp0=arr("L0_conv_w_proj").T,
        wq1=arr("L1_conv_q_w"), wk1=arr("L1_conv_k_w"), wv1=arr("L1_conv_v_w"), wp1=arr("L1_conv_proj_w").T,
        vectors=_np.stack([column(a) for a in vectors], axis=1),
        ident=_np.eye(P, dtype=_np.float32), gmean=gmean)
    nc = _bacc.Bacc("TRN2", target_bir_lowering=False, num_devices=1)
    arrays, args = {}, {}
    for name, a in given.items():
        a = _np.ascontiguousarray(a)
        arrays[f"in_{name}"] = a
        args[name] = nc.dram_tensor(f"in_{name}", a.shape, _mybir.dt.from_np(a.dtype), kind="ExternalInput").ap()
    args["out"] = nc.dram_tensor("out_x", (B, P, KT, N), _mybir.dt.float32, kind="ExternalOutput").ap()
    attention_blocks(nc, **args)
    r = _run(nc, [arrays], core_ids=[0])
    got = r.results[0]["out_x"]
    return _np.ascontiguousarray(got.transpose(0, 2, 1, 3)).reshape(B, C, 32, 32)
```
